# Optimizing a Trainium2 kernel written in Bass

```python
import numpy as np
import jax
import jax.numpy as jnp

def _softmax(x, axis=-1):
    return jax.nn.softmax(x, axis=axis)

def _gelu(x):
    return jax.nn.gelu(x, approximate=True)

def _silu(x):
    return jax.nn.silu(x)

def _sigmoid(x):
    return jax.nn.sigmoid(x)

def _layernorm(x, axis=-1, eps=1e-05):
    m = jnp.mean(x, axis=axis, keepdims=True)
    v = jnp.var(x, axis=axis, keepdims=True)
    return (x - m) / jnp.sqrt(v + eps)

def _scatter_add(tgt, idx, src, axis=0):
    return tgt.at[idx].add(src)

def _segment_sum(src, seg, n):
    return jax.ops.segment_sum(src, seg, n)
kernel_name = 'mk_gnn_resnorm_d2_gnn_r8_4245ea'

def setup_inputs(seed: int=0):
    np.random.seed(seed)
    _w = jnp.asarray

    def _rec_inputs():
        import jax
        import jax.numpy as jnp
        _gk = jax.random.key(seed)
        x = -0.000202 + 1 * jax.random.normal(jax.random.fold_in(_gk, 1), (6250, 128), jnp.float32)
        _s = jax.random.randint(jax.random.fold_in(_gk, 2), (50000,), 0, 6250, jnp.int32)
        _d = jax.random.randint(jax.random.fold_in(_gk, 3), (50000,), 0, 6250, jnp.int32)
        _loop = jnp.arange(6250, dtype=jnp.int32)
        src = jnp.concatenate([_s, _d, _loop])
        dst = jnp.concatenate([_d, _s, _loop])
        _o = jnp.argsort(dst, stable=True)
        src = src[_o]
        dst = dst[_o]
        edge_attr_20 = -8.62073e-06 + 0.999901 * jax.random.normal(jax.random.fold_in(_gk, 12), (106250, 20), jnp.float32)
        edge_weight = jax.random.uniform(jax.random.fold_in(_gk, 14), (106250,), jnp.float32, 0.0, 0.999999)
        return (x, src, dst, edge_attr_20, edge_weight)
    x, src, dst, edge_attr_20, edge_weight = _rec_inputs()

    def _L0_gnn_setup():
        import jax, jax.numpy as jnp
        import numpy as np
        N, E, D = (6250, 100000, 128)
        H = 2 * D
        L = 3
        key = jax.random.key(seed)
        ks = jax.random.split(key, 12)
        g = lambda k, shape: jax.random.normal(k, shape, jnp.float32) * 0.05
        return {'x': jax.random.normal(ks[0], (N, D), jnp.float32), 'edge_index': jax.random.randint(ks[1], (2, E), 0, N), 'phi_w1': g(ks[2], (L, 2 * D, H)), 'phi_b1': g(ks[3], (L, H)), 'phi_w2': g(ks[4], (L, H, D)), 'phi_b2': g(ks[5], (L, D)), 'psi_w1': g(ks[6], (L, D, H)), 'psi_b1': g(ks[7], (L, H)), 'psi_w2': g(ks[8], (L, H, D)), 'psi_b2': g(ks[9], (L, D)), 'proj_w': g(ks[10], (D, D)), 'proj_b': g(ks[11], (D,))}
    _L0_gnn_all = _L0_gnn_setup()
    _L0_gnn_in = {k: v for k, v in _L0_gnn_all.items() if k in ('phi_w1', 'phi_b1', 'phi_w2', 'phi_b2', 'psi_w1', 'psi_b1', 'psi_w2', 'psi_b2', 'proj_w', 'proj_b')}
    del _L0_gnn_all

    def _L1_gnn_setup():
        import jax, jax.numpy as jnp
        import numpy as np
        N_ATOMS = 6250
        N_EDGES = 200000
        N_BASIS = 128
        N_RBF = 20
        N_FILT = 128
        LOG2 = float(np.log(2.0))

        def ssp(t):
            return jax.nn.softplus(t) - LOG2
        key = jax.random.key(seed)
        ks = jax.random.split(key, 12)
        s = lambda fan_in: 1.0 / np.sqrt(fan_in)
        return {'x': jax.random.normal(ks[0], (N_ATOMS, N_BASIS), dtype=jnp.float32), 'f_ij': jax.random.normal(ks[1], (N_EDGES, N_RBF), dtype=jnp.float32), 'rcut_ij': jax.random.uniform(ks[2], (N_EDGES,), dtype=jnp.float32), 'idx_i': jnp.sort(jax.random.randint(ks[3], (N_EDGES,), 0, N_ATOMS)), 'idx_j': jax.random.randint(ks[4], (N_EDGES,), 0, N_ATOMS), 'W_in2f': jax.random.normal(ks[5], (N_BASIS, N_FILT), dtype=jnp.float32) * s(N_BASIS), 'W_f1': jax.random.normal(ks[6], (N_RBF, N_FILT), dtype=jnp.float32) * s(N_RBF), 'b_f1': jnp.zeros((N_FILT,), dtype=jnp.float32), 'W_f2': jax.random.normal(ks[7], (N_FILT, N_FILT), dtype=jnp.float32) * s(N_FILT), 'b_f2': jnp.zeros((N_FILT,), dtype=jnp.float32), 'W_o1': jax.random.normal(ks[8], (N_FILT, N_BASIS), dtype=jnp.float32) * s(N_FILT), 'b_o1': jnp.zeros((N_BASIS,), dtype=jnp.float32), 'W_o2': jax.random.normal(ks[9], (N_BASIS, N_BASIS), dtype=jnp.float32) * s(N_BASIS), 'b_o2': jnp.zeros((N_BASIS,), dtype=jnp.float32)}
    _L1_gnn_all = _L1_gnn_setup()
    _L1_gnn_in = {k: v for k, v in _L1_gnn_all.items() if k in ('W_in2f', 'W_f1', 'b_f1', 'W_f2', 'b_f2', 'W_o1', 'b_o1', 'W_o2', 'b_o2')}
    del _L1_gnn_all
    return {'x': x, 'src': src, 'dst': dst, 'edge_attr_20': edge_attr_20, 'edge_weight': edge_weight, 'L0_gnn_phi_w1': _L0_gnn_in['phi_w1'], 'L0_gnn_phi_b1': _L0_gnn_in['phi_b1'], 'L0_gnn_phi_w2': _L0_gnn_in['phi_w2'], 'L0_gnn_phi_b2': _L0_gnn_in['phi_b2'], 'L0_gnn_psi_w1': _L0_gnn_in['psi_w1'], 'L0_gnn_psi_b1': _L0_gnn_in['psi_b1'], 'L0_gnn_psi_w2': _L0_gnn_in['psi_w2'], 'L0_gnn_psi_b2': _L0_gnn_in['psi_b2'], 'L0_gnn_proj_w': _L0_gnn_in['proj_w'], 'L0_gnn_proj_b': _L0_gnn_in['proj_b'], 'L1_gnn_W_in2f': _L1_gnn_in['W_in2f'], 'L1_gnn_W_f1': _L1_gnn_in['W_f1'], 'L1_gnn_b_f1': _L1_gnn_in['b_f1'], 'L1_gnn_W_f2': _L1_gnn_in['W_f2'], 'L1_gnn_b_f2': _L1_gnn_in['b_f2'], 'L1_gnn_W_o1': _L1_gnn_in['W_o1'], 'L1_gnn_b_o1': _L1_gnn_in['b_o1'], 'L1_gnn_W_o2': _L1_gnn_in['W_o2'], 'L1_gnn_b_o2': _L1_gnn_in['b_o2']}

def reference(x, src, dst, edge_attr_20, edge_weight, L0_gnn_phi_w1, L0_gnn_phi_b1, L0_gnn_phi_w2, L0_gnn_phi_b2, L0_gnn_psi_w1, L0_gnn_psi_b1, L0_gnn_psi_w2, L0_gnn_psi_b2, L0_gnn_proj_w, L0_gnn_proj_b, L1_gnn_W_in2f, L1_gnn_W_f1, L1_gnn_b_f1, L1_gnn_W_f2, L1_gnn_b_f2, L1_gnn_W_o1, L1_gnn_b_o1, L1_gnn_W_o2, L1_gnn_b_o2):
    import jax
    import jax.numpy as jnp

    def _L0_gnn_ref(x, edge_index, phi_w1, phi_b1, phi_w2, phi_b2, psi_w1, psi_b1, psi_w2, psi_b2, proj_w, proj_b):
        import jax, jax.numpy as jnp
        import numpy as np
        N, E, D = (6250, 100000, 128)
        H = 2 * D
        L = 3
        relu = jax.nn.relu

        def mlp(h, w1, b1, w2, b2):
            return relu(h @ w1 + b1) @ w2 + b2
        src, dst = (edge_index[0], edge_index[1])
        n = x.shape[0]
        deg = jax.ops.segment_sum(jnp.ones((edge_index.shape[1],), x.dtype), dst, num_segments=n)
        deg = jnp.maximum(deg, 1.0)[:, None]

        def conv(h, l):
            x_i = h[dst]
            x_j = h[src]
            m = mlp(jnp.concatenate([x_i, x_j - x_i], axis=1), phi_w1[l], phi_b1[l], phi_w2[l], phi_b2[l])
            agg = jax.ops.segment_sum(m, dst, num_segments=n) / deg
            return mlp(agg, psi_w1[l], psi_b1[l], psi_w2[l], psi_b2[l])
        pr = x @ proj_w + proj_b
        h = relu(conv(x, 0)) + pr
        h = relu(conv(h, 1)) + h
        return conv(h, 2)

    def _L1_gnn_ref(x, f_ij, rcut_ij, idx_i, idx_j, W_in2f, W_f1, b_f1, W_f2, b_f2, W_o1, b_o1, W_o2, b_o2):
        import jax, jax.numpy as jnp
        import numpy as np
        N_ATOMS = 6250
        N_EDGES = 200000
        N_BASIS = 128
        N_RBF = 20
        N_FILT = 128
        LOG2 = float(np.log(2.0))

        def ssp(t):
            return jax.nn.softplus(t) - LOG2
        n_atoms = x.shape[0]
        h = x @ W_in2f
        Wij = ssp(f_ij @ W_f1 + b_f1) @ W_f2 + b_f2
        Wij = Wij * rcut_ij[:, None]
        x_ij = h[idx_j] * Wij
        agg = jax.ops.segment_sum(x_ij, idx_i, num_segments=n_atoms)
        out = ssp(agg @ W_o1 + b_o1) @ W_o2 + b_o2
        return out
    edge_index = jnp.stack([src, dst])
    x = _layernorm(x + _L0_gnn_ref(x, edge_index, L0_gnn_phi_w1, L0_gnn_phi_b1, L0_gnn_phi_w2, L0_gnn_phi_b2, L0_gnn_psi_w1, L0_gnn_psi_b1, L0_gnn_psi_w2, L0_gnn_psi_b2, L0_gnn_proj_w, L0_gnn_proj_b), axis=-1)
    x = _layernorm(x + _L1_gnn_ref(x, edge_attr_20, edge_weight, src, dst, L1_gnn_W_in2f, L1_gnn_W_f1, L1_gnn_b_f1, L1_gnn_W_f2, L1_gnn_b_f2, L1_gnn_W_o1, L1_gnn_b_o1, L1_gnn_W_o2, L1_gnn_b_o2), axis=-1)
    return x

_drawn_inputs = setup_inputs


def setup_inputs(seed=0):
    import zlib

    import numpy as np

    out = dict(_drawn_inputs(seed))
    spreads = {'L1_gnn_b_f1': (0.0, 0.1),
     'L1_gnn_b_f2': (0.0, 0.1),
     'L1_gnn_b_o1': (0.0, 0.1),
     'L1_gnn_b_o2': (0.0, 0.1)}
    factors = {'L0_gnn_phi_b1': 7.113, 'L0_gnn_phi_b2': 3.293, 'L0_gnn_proj_b': 8.0}
    for name, (base, spread) in spreads.items():
        noise = np.random.default_rng([zlib.crc32(name.encode()), seed]).standard_normal(out[name].shape)
        drawn = base * np.exp(spread * noise) if base else spread * noise
        out[name] = jnp.asarray(drawn.astype(out[name].dtype))
    for name, factor in factors.items():
        out[name] = (out[name] * factor).astype(out[name].dtype)
    return out
```

```python
import numpy as np
import concourse.bass as bass
from concourse import mybir
from contextlib import ExitStack

F32 = mybir.dt.float32
BF16 = mybir.dt.bfloat16
I32 = mybir.dt.int32
ALU = mybir.AluOpType
ACT = mybir.ActivationFunctionType

P = 128
NODES, EDGES, D, H, RBF, LAYERS = 6250, 106250, 128, 256, 20, 3
TILES = 4
GROUP = TILES * P
UNROLL = 4
GROUPS = -(-EDGES // (GROUP * UNROLL)) * UNROLL
AHEAD = 4
TABLE = (GROUPS + AHEAD) * TILES
WIN = 42
WIN3 = 3 * WIN
CHUNK = 512
CHUNKS = -(-NODES // CHUNK)
NPAD = CHUNK * CHUNKS
CT = CHUNK // P
NB = -(-NODES // P)
STEP = 8
STEPS = GROUPS * TILES // STEP
SORTED = -(-(GROUPS * TILES + NB) // (TILES * UNROLL)) * TILES * UNROLL
TAIL = SORTED - GROUPS * TILES
SPARE = SORTED + NB
ROW = D + 1
LOG2 = float(np.log(2.0))
EPS = 1e-5
FULL_TILES, REST = NODES // P, NODES % P


def build(nc, xT, xN, src, dst, rcut, fT, phi_w1, phi_b1, phi_w2, phi_b2, psi_w1, psi_b1, psi_w2,
          psi_b2, psi_b2_last, proj_w, proj_b, w_in2f, w_f1, b_f1, w_f2, b_f2, w_o1, b_o1, w_o2, b_o2, out):
    ctx = ExitStack()
    with ctx:
        def sb(name, shape, dt=F32):
            return ctx.enter_context(nc.sbuf_tensor(name, shape, dt))

        def ps(name, shape, dt=F32):
            return ctx.enter_context(nc.psum_tensor(name, shape, dt))

        def sem(name):
            return ctx.enter_context(nc.semaphore(name))

        B_d = [nc.dram_tensor(f"B_table{l}", [NPAD, H], F32, kind="Internal").ap() for l in range(LAYERS)]
        A3_d = [nc.dram_tensor(f"A_table{l}", [NPAD * 3, H], BF16, kind="Internal").ap() for l in range(LAYERS)]
        hf3_d = nc.dram_tensor("filter_table", [NPAD * 3, D], BF16, kind="Internal").ap()
        sorted_d = nc.dram_tensor("sorted_messages", [(SPARE + NB) * P, ROW], F32, kind="Internal").ap()

        w1 = sb("w1", [P, LAYERS, 2 * H])
        w2 = sb("w2", [P, LAYERS, 2, D])
        v1 = sb("v1", [P, LAYERS, H])
        v2 = sb("v2", [P, LAYERS, 2, D])
        b1_bc = sb("b1_bc", [P, LAYERS, H])
        b2_col = sb("b2_col", [P, LAYERS])
        c1_col = sb("c1_col", [P, LAYERS, 2])
        c2_col = sb("c2_col", [P, LAYERS])
        c2_bc = sb("c2_bc", [P, D])
        pw = sb("pw", [P, D])
        pb_col = sb("pb_col", [P, 1])
        win2f = sb("win2f", [P, D])
        wf1 = sb("wf1", [RBF, D])
        wf2 = sb("wf2", [P, D])
        wo1 = sb("wo1", [P, D])
        wo2 = sb("wo2", [P, D])
        bf1_col = sb("bf1_col", [P, 1])
        bo1_col = sb("bo1_col", [P, 1])
        bo2_bc = sb("bo2_bc", [P, D])
        bf2_row = sb("bf2_row", [P, D])
        first_row = sb("first_row", [P, P])
        ones = sb("ones", [P, P])
        ident_b = sb("ident_b", [P, P], BF16)
        ident = sb("ident", [P, P])
        iota3 = sb("iota3", [P, WIN3], BF16)
        iota1 = sb("iota1", [P, WIN])

        src_t = sb("src_t", [P, TABLE], I32)
        dst_f = sb("dst_f", [P, TABLE])
        base_i = sb("base_i", [1, GROUPS + AHEAD], I32)

        iota_b = sb("iota_b", [P, NB])
        below = sb("below", [P, P], BF16)
        not_below = sb("not_below", [P, P], BF16)
        idx = sb("idx", [P, UNROLL * TILES], I32)
        G = sb("G", [P, UNROLL, TILES * H])
        A3 = sb("A3", [WIN3, UNROLL, H], BF16)
        hot3 = sb("hot3", [P, 2, TILES, WIN3], BF16)
        hotT = sb("hotT", [WIN3, 2, GROUP], BF16)
        hot = sb("hot", [P, UNROLL, TILES, WIN])
        M = sb("M", [P, 2, TILES * H])
        agg = sb("agg", [P, 3, NPAD])
        inv = sb("inv", [P, NPAD])
        hT = sb("hT", [P, NPAD])
        st4 = sb("st4", [P, CT, 6])
        stats = sb("stats", [P, CHUNKS * CT, 6])
        mean = sb("mean", [P, CHUNKS * CT])
        zeros = sb("zeros", [P, 1])
        veps = sb("veps", [P, CHUNKS * CT])
        std = sb("std", [P, CHUNKS * CT])
        rstd = sb("rstd", [P, CHUNKS * CT])
        x1 = inv[:, :].rearrange("p (t d) -> p t d", d=D)
        m_b = G[:, 0, 0:CHUNK]
        t_b = G[:, 0, CHUNK:2 * CHUNK]
        u_b = G[:, 1, :].rearrange("p (h n) -> p h n", h=2)
        r_b = G[:, 2, 0:CHUNK]
        xres = G[:, 2, CHUNK:2 * CHUNK]
        h_b = G[:, 3, 0:CHUNK]
        x_b = G[:, 3, CHUNK:2 * CHUNK]
        xres_t = xres.rearrange("p (t d) -> p t d", d=D)
        Bst = M[:, :, 0:2 * H].rearrange("p s (t f) -> p s t f", t=2)
        Af = M[:, 0, 2 * H:4 * H].rearrange("p (t f) -> p t f", t=2)
        Ar = M[:, 1, 2 * H:4 * H].rearrange("p (t f) -> p t f", t=2)
        A3st = sb("A3st", [P, 2, 2, 3, H], BF16)
        H3st = A3st[:, 0, :, :, :].rearrange("p t c f -> p (t c f)").rearrange(
            "p (t c f) -> p t c f", t=CT, c=3)
        y_b = x_b
        zone = agg[:, 1:3, :].rearrange("p a n -> p (a n)")
        taken = [0]

        def part(n, dt=F32):
            at = taken[0]
            taken[0] += n
            assert taken[0] <= 2 * NPAD
            words = zone[:, at:at + n]
            return words if dt == F32 else words.bitcast(dt)

        bucket_f = part(GROUPS * TILES)
        place_f = part(GROUPS * TILES)
        one_bucket = part(STEP * NB).bitcast(BF16).rearrange("p (s t b) -> p s t b", s=2, t=STEP)
        picked = part(STEP * NB).rearrange("p (t b) -> p t b", b=NB)
        many = part(NB)
        tiles_b, ends, ends2, starts, full = part(NB), part(NB), part(NB), part(NB), part(NB)
        tiles_i = part(NB, I32)
        zero_list_f = part(NB + TAIL)
        col_end = part(1)
        taken[0] = 0
        fbuf = part(UNROLL * GROUP)[0:RBF, :].rearrange("p (s e) -> p s e", s=UNROLL)
        a_b, e_b, l_b, q_b = part(GROUP), part(GROUP), part(GROUP), part(GROUP)
        sp_b = part(2 * GROUP).rearrange("p (s e) -> p s e", s=2)
        xj_b = part(2 * GROUP).rearrange("p (s e) -> p s e", s=2)
        rcut_t = part(TABLE)
        loc_f = part(GROUPS * TILES)
        place_i = part(GROUPS * TILES, I32)
        iota_t = part(SORTED)
        zero_rows = part(ROW)
        zero_list = part(NB + TAIL, I32)
        node_base = part(SORTED, I32)
        ends_last = [ends, ends2][(NB - 1).bit_length() % 2 - 1]
        rows = G[:, :, 0:TILES * ROW].rearrange("p u (t w) -> p u t w", w=ROW)
        hot128 = M[:, :, 0:TILES * P].rearrange("p s (t n) -> p s t n", n=P)

        PX = ps("PX", [P, 4, 512])
        PO = ps("PO", [P, 2, 512])
        PT = ps("PT", [P, 2, 512])
        PTb = [PT[:, s, :].bitcast(BF16) for s in range(2)]
        tab_bank = [PO, PT]

        s_w = sem("weights_in")
        s_tab = sem("edge_tables_in")
        s_pool0 = sem("pool_constants")
        s_c = sem("vector_constants")
        s_bb = sem("bases_spread")
        s_idx = sem("indices_staged")
        s_G = [sem(f"rows_gathered{i}") for i in range(UNROLL)]
        s_win = [sem(f"window_in{i}") for i in range(UNROLL)]
        s_hot = sem("hot_built")
        s_tr = sem("hot_transposed")
        s_hotT = sem("hotT_ready")
        s_X = sem("A_spread")
        s_add = sem("pre_relu_ready")
        s_M = sem("messages_ready")
        s_seg = sem("messages_summed")
        s_acc = sem("agg_added")
        s_zero = sem("agg_zeroed")
        s_z = sem("z_ready")
        s_t = sem("vector_step")
        s_m = sem("mean_ready")
        s_u = sem("u_ready")
        s_ur = sem("u_relu")
        s_v = sem("v_ready")
        s_h = sem("h_ready")
        s_tp = sem("table_product")
        s_bev = sem("B_rows_copied")
        s_at = sem("A_split_step")
        s_am = sem("A_two_parts")
        s_lo = sem("A_third_part")
        s_store = [sem(f"table_stored{i}") for i in range(2)]
        s_xres = sem("x_rows_in")
        s_y = sem("y_ready")
        s_var = sem("variances_ready")
        s_std = sem("std_ready")
        s_x1 = sem("x1_ready")
        s_x1p = sem("x1_transposed")
        s_x1T = sem("x1T_copied")
        s_keep = sem("features_kept")
        s_nx = sem("x1_normed")
        s_bn = sem("statistics_step")
        s_nt = sem("newton_step")
        s_ot = sem("output_vector_step")
        s_hf = sem("hf_product")
        s_hs = sem("hf_split_step")
        s_hlo = sem("hf_third_part")
        s_rcut = sem("rcut_in")
        s_rt = sem("route_step")
        s_cnt = sem("bucket_counted")
        s_tot = sem("bucket_totals")
        s_start = sem("bucket_starts")
        s_run = sem("running_starts")
        s_mask = sem("tile_masks")
        s_tb = sem("tile_buckets")
        s_list = sem("lists_ready")
        s_ob = sem("bucket_hot_built")
        s_pre = sem("prefix_added")
        s_ps = sem("prefix_read")
        s_pick = sem("places_picked")
        s_cum = sem("step_added")
        s_clear = sem("gaps_cleared")
        s_place = sem("places_ready")
        s_f = [sem(f"f_in{i}") for i in range(UNROLL)]
        s_Z = sem("filter_hidden")
        s_abs = sem("abs_ready")
        s_exp = sem("exp_ready")
        s_ln = sem("ln_ready")
        s_q = sem("q_ready")
        s_sp = sem("softplus_ready")
        s_Y = sem("filter_ready")
        s_xj = sem("rows_by_edge_copied")
        s_prod = sem("x_ij_ready")
        s_row = [sem(f"sorted_in{i}") for i in range(UNROLL)]
        s_hot128 = sem("bucket_nodes_hot")
        s_seg1 = sem("x_ij_summed")
        s_acc1 = sem("agg1_added")
        s_o1 = sem("o1_ready")
        s_oa = sem("o_act_step")
        s_osp = sem("o_softplus")
        s_o2 = sem("o2_ready")
        s_y2 = sem("y2_ready")
        s_norm = sem("rows_normed")
        s_out = sem("rows_out")

        N_W = 24

        block = ctx.enter_context(nc.Block())
        chunk = lambda k: bass.ds(k * CHUNK, CHUNK)

        @block.sync
        def _(sp):
            sp.dma_start(src_t[:, :], src).then_inc(s_tab, 16)
            sp.dma_start(G[:, 0, 0:TABLE].bitcast(I32), dst).then_inc(s_tab, 16)
            sp.dma_start(hT[:, :], xT).then_inc(s_tab, 16)
            loads = [
                (w1[:, :, 0:H], phi_w1[:, 0:P, :].rearrange("l p f -> p l f")),
                (w1[:, :, H:2 * H], phi_w1[:, P:2 * P, :].rearrange("l p f -> p l f")),
                (b1_bc[:, :, :], phi_b1.rearrange("(a l) f -> a l f", a=1).to_broadcast([P, LAYERS, H])),
                (v1[:, :, :], psi_w1.rearrange("l p f -> p l f")),
                (b2_col[:, :], phi_b2), (c2_col[:, :], psi_b2),
                (c1_col[:, :, :], psi_b1),
                (pw[:, :], proj_w), (pb_col[:, :], proj_b),
                (win2f[:, :], w_in2f), (wf1[:, :], w_f1), (wf2[:, :], w_f2),
                (wo1[:, :], w_o1), (wo2[:, :], w_o2), (bf1_col[:, :], b_f1), (bo1_col[:, :], b_o1),
                (bo2_bc[:, :], b_o2.to_broadcast([P, D])),
                (c2_bc[:, :], psi_b2_last.to_broadcast([P, D])),
            ]
            for l in range(LAYERS):
                loads.append((w2[:, l, :, :], phi_w2[l].rearrange("(h p) d -> p h d", p=P)))
                loads.append((v2[:, l, :, :], psi_w2[l].rearrange("(h p) d -> p h d", p=P)))
            assert len(loads) == N_W
            for to, of in loads:
                sp.dma_start(to, of).then_inc(s_w, 16)
            sp.wait_ge(s_pool0, 1)
            sp.dma_start(bf2_row[0:1, :], b_f2).then_inc(s_w, 16)

            def store_tables(n, k):
                for half in range(2):
                    q = (n * CHUNKS + k) * 2 + half
                    r = k * CT + 2 * half
                    sp.wait_ge(s_bev, q + 1)
                    sp.dma_start(B_d[n][bass.ds(r * P, 2 * P), :].rearrange("(t p) f -> p t f", p=P),
                                 Bst[:, half, :, :]).then_inc(s_store[half], 16)
                    sp.wait_ge(s_am, q + 1)
                    sp.wait_ge(s_lo, q + 1)
                    sp.dma_start(A3_d[n][bass.ds(r * P * 3, 2 * P * 3), :].rearrange(
                                     "(t p c) f -> p t (c f)", p=P, c=3),
                                 A3st[:, half, :, :, :].rearrange("p t c f -> p t (c f)")
                                 ).then_inc(s_store[half], 16)

            def stored(eng, n):
                for half in range(2):
                    eng.wait_ge(s_store[half], (n + 1) * CHUNKS * 32)

            def load_window(l, g, u):
                c = l * GROUPS + g
                if not (isinstance(c, int) and c < UNROLL):
                    sp.wait_ge(s_X, c - UNROLL + 1)
                b = sp.value_load(base_i[0:1, bass.ds(g, 1)], min_val=0, max_val=NODES)
                table, width = (A3_d[l], H) if l < LAYERS else (hf3_d, D)
                sp.dma_start(A3[:, u, 0:width], table[bass.ds(b * 3, WIN3), :]).then_inc(s_win[u], 16)

            with nc.allow_non_contiguous_dma(reason="rows of a table"):
                with sp.Fori(0, CHUNKS, 1) as k:
                    store_tables(0, k)
                sp.wait_ge(s_c, 6)
                for l in range(LAYERS):
                    stored(sp, l)
                    for u in range(UNROLL):
                        load_window(l, u, u)
                    with sp.Fori(1, GROUPS // UNROLL, 1) as i:
                        for u in range(UNROLL):
                            load_window(l, i * UNROLL + u, u)
                    if l < LAYERS - 1:
                        with sp.Fori(0, CHUNKS, 1) as k:
                            store_tables(l + 1, k)
                sp.wait_ge(s_acc, LAYERS * GROUPS)
                with sp.Fori(0, CHUNKS, 1) as k:
                    sp.wait_ge(s_m, (LAYERS - 1) * CHUNKS + k + 1)
                    sp.dma_start(xres.rearrange("p (t d) -> p t d", d=D),
                                 xN[chunk(k), :].rearrange("(t p) d -> p t d", p=P)).then_inc(s_xres, 16)
                with sp.Fori(0, CHUNKS, 1) as k:
                    sp.wait_ge(s_hlo, k + 1)
                    sp.dma_start(hf3_d[bass.ds(k * CHUNK * 3, CHUNK * 3), :].rearrange(
                                     "(t p c) f -> p t (c f)", p=P, c=3),
                                 H3st.rearrange("p t c f -> p t (c f)")).then_inc(s_xres, 16)
                sp.dma_start(rcut_t, rcut).then_inc(s_rcut, 16)
                sp.wait_ge(s_list, 1)
                with sp.Fori(0, NB + TAIL, 1) as n:
                    tile = sp.value_load(zero_list[0:1, bass.ds(n, 1)], min_val=0, max_val=SPARE + NB - 1)
                    sp.dma_start(sorted_d[bass.ds(tile * P, P), :], zero_rows).then_inc(s_clear, 16)

                def load_f(i, u):
                    g = i * UNROLL + u
                    if not (isinstance(g, int) and g < UNROLL):
                        sp.wait_ge(s_Z, g - UNROLL + 1)
                    sp.dma_start(fbuf[:, u, :], fT[:, bass.ds(g * GROUP, GROUP)]).then_inc(s_f[u], 16)

                sp.wait_ge(s_xres, 32 * CHUNKS)
                sp.wait_ge(s_place, 1)
                for u in range(UNROLL):
                    load_f(0, u)
                    load_window(LAYERS, u, u)
                with sp.Fori(1, GROUPS // UNROLL, 1) as i:
                    for u in range(UNROLL):
                        load_f(i, u)
                        load_window(LAYERS, i * UNROLL + u, u)
                load_f(GROUPS // UNROLL, 0)

                def load_rows(i, u):
                    g = i * UNROLL + u
                    if not (isinstance(g, int) and g < UNROLL):
                        sp.wait_ge(s_seg1, g - UNROLL + 1)
                    sp.dma_start(rows[:, u, :, :], sorted_d[bass.ds(g * GROUP, GROUP), :].rearrange(
                        "(t p) w -> p t w", p=P)).then_inc(s_row[u], 16)

                for u in range(UNROLL):
                    sp.wait_ge(s_G[u], (LAYERS + 1) * (GROUPS // UNROLL) * TILES * 16)
                sp.wait_ge(s_clear, 16 * (NB + TAIL))
                for u in range(UNROLL):
                    load_rows(0, u)
                with sp.Fori(1, SORTED // TILES // UNROLL, 1) as i:
                    for u in range(UNROLL):
                        load_rows(i, u)

                with sp.Fori(0, FULL_TILES // CT, 1) as k:
                    sp.wait_ge(s_norm, k + 1)
                    sp.dma_start(out[chunk(k), :].rearrange("(t p) d -> p t d", p=P),
                                 x1[:, bass.ds(k * CT, CT), :]).then_inc(s_out, 16)
                sp.wait_ge(s_norm, CHUNKS)
                sp.dma_start(out[FULL_TILES * P:NODES, :], x1[0:REST, FULL_TILES, :]).then_inc(s_out, 16)
                sp.wait_ge(s_out, 16 * CHUNKS)

        @block.gpsimd
        def _(pool):
            pool.memset(bf2_row[:, :], 0.0).then_inc(s_pool0, 1)
            pool.memset(first_row[:, :], 0.0).then_inc(s_pool0, 1)
            pool.memset(ident[:, :], 0.0).then_inc(s_pool0, 1)
            pool.memset(ones[:, :], 1.0).then_inc(s_pool0, 1)
            pool.iota(iota1[:, :], pattern=[[1, WIN]], base=0, channel_multiplier=0,
                      allow_small_or_imprecise_dtypes=True).then_inc(s_pool0, 1)
            pool.iota(iota3[:, :], pattern=[[1, WIN], [0, 3]], base=0, channel_multiplier=0,
                      allow_small_or_imprecise_dtypes=True).then_inc(s_pool0, 1)
            pool.memset(zeros[:, :], 0.0).then_inc(s_pool0, 1)
            pool.iota(iota_b[:, :], pattern=[[1, NB]], base=0, channel_multiplier=0,
                      allow_small_or_imprecise_dtypes=True).then_inc(s_pool0, 1)
            pool.memset(below[:, :], 1.0).then_inc(s_pool0, 1)
            pool.memset(not_below[:, :], 1.0).then_inc(s_pool0, 1)
            pool.wait_ge(s_pool0, 10)
            pool.affine_select(out=below[:, :], in_=below[:, :], compare_op=ALU.is_ge, fill=0.0,
                               base=-1, pattern=[[1, P]], channel_multiplier=-1).then_inc(s_pool0, 1)
            pool.affine_select(out=not_below[:, :], in_=not_below[:, :], compare_op=ALU.is_ge, fill=0.0,
                               base=0, pattern=[[-1, P]], channel_multiplier=1).then_inc(s_pool0, 1)
            pool.affine_select(out=ident[:, :], in_=ident[:, :], compare_op=ALU.not_equal, fill=1.0,
                               base=0, pattern=[[-1, P]], channel_multiplier=1).then_inc(s_pool0, 1)
            pool.memset(first_row[0:1, :], 1.0).then_inc(s_pool0, 1)
            pool.memset(agg[:, :, :], 0.0).then_inc(s_zero, 1)

            last_row = pool.alloc_register("last_row")
            row_before = pool.alloc_register("row_before")
            pool.reg_mov(row_before, NPAD - 2)

            def third_part(n, k):
                for half in range(2):
                    q = (n * CHUNKS + k) * 2 + half
                    pool.wait_ge(s_am, q + 1)
                    pool.tensor_tensor(out=A3st[:, half, :, 2, :], in0=Ar, in1=A3st[:, half, :, 1, :],
                                       op=ALU.subtract).then_inc(s_lo, 1)

            def rows_in_out(l, i):
                for u in range(UNROLL):
                    c = l * GROUPS + i * UNROLL + u
                    if u % 2 == 0:
                        pool.wait_ge(s_idx, l * (GROUPS // 2) + i * 2 + u // 2 + (1 if l < LAYERS else 3))
                    if l < LAYERS and not (isinstance(c, int) and c < UNROLL):
                        pool.wait_ge(s_add, c - UNROLL + 1)
                    if l == LAYERS:
                        pool.wait_ge(s_prod, i * UNROLL + u + 1)
                    pool.reg_add(last_row, row_before, 1)
                    for j in range(TILES):
                        at = bass.IndirectOffsetOnAxis(ap=idx[:, u * TILES + j:u * TILES + j + 1], axis=0)
                        if l < LAYERS:
                            pool.indirect_dma_start(
                                out=G[:, u, j * H:(j + 1) * H], out_offset=None, in_=B_d[l][:, :], in_offset=at,
                                bounds_check=last_row, oob_is_err=False).then_inc(s_G[u], 16)
                        else:
                            pool.indirect_dma_start(
                                out=sorted_d[:, :], out_offset=at, in_=rows[:, u, j, :], in_offset=None,
                                bounds_check=last_row, oob_is_err=False).then_inc(s_G[u], 16)

            with pool.Fori(0, CHUNKS, 1) as k:
                third_part(0, k)
            for l in range(LAYERS):
                for half in range(2):
                    pool.wait_ge(s_store[half], (l + 1) * CHUNKS * 32)
                rows_in_out(l, 0)
                with pool.Fori(1, GROUPS // UNROLL, 1) as i:
                    rows_in_out(l, i)
                if l < LAYERS - 1:
                    with pool.Fori(0, CHUNKS, 1) as k:
                        pool.wait_ge(s_z, l * CHUNKS + k + 1)
                        pool.tensor_copy(agg[:, 0, chunk(k)], zeros[:, 0:1].to_broadcast([P, CHUNK])).then_inc(s_zero, 1)
                        pool.tensor_copy(agg[:, 1, chunk(k)], zeros[:, 0:1].to_broadcast([P, CHUNK])).then_inc(s_zero, 1)
                        if l == 0:
                            pool.wait_ge(s_h, CHUNKS + k + 1)
                            pool.tensor_copy(hT[:, chunk(k)], h_b).then_inc(s_keep, 1)
                        third_part(l + 1, k)
            with pool.Fori(0, CHUNKS, 1) as k:
                pool.wait_ge(s_z, (LAYERS - 1) * CHUNKS + k + 1)
                pool.tensor_copy(agg[:, 0, chunk(k)], zeros[:, 0:1].to_broadcast([P, CHUNK])).then_inc(s_zero, 1)
            pool.iota(iota_t, pattern=[[1, SORTED]], base=0, channel_multiplier=0,
                      allow_small_or_imprecise_dtypes=True).then_inc(s_zero, 1)
            pool.memset(zero_rows, 0.0).then_inc(s_zero, 1)
            with pool.Fori(0, CHUNKS, 1) as k:
                pool.wait_ge(s_hs, 3 * k + 3)
                pool.tensor_tensor(out=H3st[:, :, 2, :], in0=xres_t, in1=H3st[:, :, 1, :],
                                   op=ALU.subtract).then_inc(s_hlo, 1)
            pool.wait_ge(s_clear, 16 * (NB + TAIL))
            pool.reg_mov(row_before, (SPARE + NB) * P - 2)
            rows_in_out(LAYERS, 0)
            with pool.Fori(1, GROUPS // UNROLL, 1) as i:
                rows_in_out(LAYERS, i)

        @block.scalar
        def _(act):
            act.preload_act_table_set("natural_log_exp_and_others")
            act.wait_ge(s_w, 16 * (N_W + 1))
            act.wait_ge(s_c, 6)

            def copy_B(n, k):
                for half in range(2):
                    q = (n * CHUNKS + k) * 2 + half
                    act.wait_ge(s_at, 3 * q + 1)
                    if not (isinstance(q, int) and q < 2):
                        act.wait_ge(s_store[half], (n * CHUNKS + k) * 32)
                    act.activation(Bst[:, half, :, :], tab_bank[half][:, :, H:2 * H], ACT.Copy).then_inc(s_bev, 1)

            def hotT_copy(c, s):
                act.wait_ge(s_tr, c + 1)
                if not (isinstance(c, int) and c < 2):
                    act.wait_ge(s_X, c - 1)
                act.activation(hotT[:, s, :], PTb[s][0:WIN3, 0:GROUP], ACT.Copy).then_inc(s_hotT, 1)

            def edge_step(l, g, u):
                c = l * GROUPS + g
                hotT_copy(c + 1, (u + 1) % 2)
                act.wait_ge(s_add, c + 1)
                act.activation(M[:, u % 2, :], M[:, u % 2, :], ACT.Relu).then_inc(s_M, 1)

            copy_B(0, 0)
            with act.Fori(1, CHUNKS, 1) as k:
                copy_B(0, k)
            hotT_copy(0, 0)
            for l in range(LAYERS):
                for u in range(UNROLL):
                    edge_step(l, u, u)
                with act.Fori(1, GROUPS // UNROLL, 1) as i:
                    for u in range(UNROLL):
                        edge_step(l, i * UNROLL + u, u)
                with act.Fori(0, CHUNKS, 1) as k:
                    kk = l * CHUNKS + k
                    act.wait_ge(s_u, kk + 1)
                    act.activation(u_b[:, 0, :], PX[:, 1, :], ACT.Relu, bias=c1_col[:, l, 0:1]).then_inc(s_ur, 1)
                    act.activation(u_b[:, 1, :], PX[:, 2, :], ACT.Relu, bias=c1_col[:, l, 1:2]).then_inc(s_ur, 1)
                    if l < LAYERS - 1:
                        copy_B(l + 1, k)
            act.wait_ge(s_var, 1)
            act.activation(std[:, :], veps[:, :], ACT.Sqrt).then_inc(s_std, 1)
            act.preload_act_table_set("natural_log_exp_and_others")
            with act.Fori(0, CHUNKS, 1) as k:
                act.wait_ge(s_x1p, k + 1)
                act.activation(m_b, PX[:, 0, :], ACT.Copy).then_inc(s_x1T, 1)
            def softplus_parts(c, s):
                act.wait_ge(s_Z, c + 1)
                act.activation(a_b, PX[:, s, :], ACT.Abs, bias=bf1_col[:, 0:1]).then_inc(s_abs, 1)
                act.wait_ge(s_abs, c + 1)
                act.activation(e_b, a_b, ACT.Exp, scale=-1.0).then_inc(s_exp, 1)
                act.wait_ge(s_exp, c + 1)
                if not (isinstance(c, int) and c < 1):
                    act.wait_ge(s_sp, c)
                act.activation(l_b, e_b, ACT.Ln, bias=1.0).then_inc(s_ln, 1)

            def filter_step(i, u):
                g = i * UNROLL + u
                hotT_copy(LAYERS * GROUPS + g + 1, (u + 1) % 2)
                act.wait_ge(s_X, LAYERS * GROUPS + g + 1)
                if not (isinstance(g, int) and g < 2):
                    act.wait_ge(s_prod, g - 1)
                act.activation(xj_b[:, u % 2, :], PO[:, u % 2, :], ACT.Copy).then_inc(s_xj, 1)
                softplus_parts(g + 1, (u + 1) % 2)

            act.wait_ge(s_place, 1)
            softplus_parts(0, 0)
            for u in range(UNROLL):
                filter_step(0, u)
            with act.Fori(1, GROUPS // UNROLL, 1) as i:
                for u in range(UNROLL):
                    filter_step(i, u)
            with act.Fori(0, CHUNKS, 1) as k:
                act.wait_ge(s_o1, k + 1)
                act.activation(m_b, PX[:, 0, :], ACT.Abs, bias=bo1_col[:, 0:1]).then_inc(s_oa, 1)
                act.wait_ge(s_oa, 3 * k + 1)
                act.activation(t_b, m_b, ACT.Exp, scale=-1.0).then_inc(s_oa, 1)
                act.wait_ge(s_oa, 3 * k + 2)
                act.activation(xres, t_b, ACT.Ln, bias=1.0).then_inc(s_oa, 1)
            act.wait_ge(s_var, 2)
            act.activation(std[:, :], veps[:, :], ACT.Sqrt).then_inc(s_std, 1)

        @block.tensor
        def _(pe):
            pe.wait_ge(s_w, 16 * (N_W + 1))
            pe.wait_ge(s_pool0, 14)
            pe.wait_ge(s_c, 3)
            last = pe.matmul(PX[:, 0, 0:GROUPS + AHEAD], first_row[:, :], dst_f[:, 0:TABLE:TILES],
                             start=True, stop=True).then_inc(s_bb, 1)

            def tables(n, k):
                pe.wait_ge(s_h, n * CHUNKS + k + 1)
                for half in range(2):
                    q = (n * CHUNKS + k) * 2 + half
                    if not (isinstance(q, int) and q < 2):
                        pe.wait_ge(s_bev, q - 1)
                        pe.wait_ge(s_am, q - 1)
                    for t in range(2):
                        mm = pe.matmul(tab_bank[half][:, t, :],
                                       h_b[:, (2 * half + t) * P:(2 * half + t + 1) * P],
                                       w1[:, n, :], start=True, stop=True)
                    mm.then_inc(s_tp, 1)

            def transposes(c, s):
                pe.wait_ge(s_hot, c + 1)
                if not (isinstance(c, int) and c < 2):
                    pe.wait_ge(s_hotT, c - 1)
                for j in range(TILES):
                    mm = pe.transpose(PTb[s][0:WIN3, j * P:(j + 1) * P], hot3[:, s, j, :], ident_b[:, :])
                mm.then_inc(s_tr, 1)

            def sum_messages(l, c, s, u4):
                pe.wait_ge(s_M, c + 1)
                if not (isinstance(c, int) and c < 2):
                    pe.wait_ge(s_acc, c - 1)
                for h in range(3 if l == 0 else 2):
                    for j in range(TILES):
                        left = ones[:, :] if h == 2 else M[:, s, j * H + h * P:j * H + (h + 1) * P]
                        mm = pe.matmul(PO[:, s, h * WIN:(h + 1) * WIN], left, hot[:, u4, j, :],
                                       start=(j == 0), stop=(j == TILES - 1))
                mm.then_inc(s_seg, 1)

            def edge_step(l, i, u, first=False):
                c = l * GROUPS + i * UNROLL + u
                pe.wait_ge(s_hotT, c + 1)
                pe.wait_ge(s_win[u], (l * (GROUPS // UNROLL) + i + 1) * 16)
                if not (isinstance(c, int) and c < 2):
                    pe.wait_ge(s_add, c - 1)
                for j in range(TILES):
                    mm = pe.matmul(PX[:, 2 * (u % 2) + j // 2, (j % 2) * H:(j % 2 + 1) * H],
                                   hotT[:, u % 2, j * P:(j + 1) * P], A3[:, u, :], start=True, stop=True)
                mm.then_inc(s_X, 1)
                transposes(c + 1, (u + 1) % 2)
                if not first:
                    sum_messages(l, c - 1, (u - 1) % 2, (u - 1) % UNROLL)

            pe.wait_ge(s_c, 6)
            tables(0, 0)
            with pe.Fori(1, CHUNKS, 1) as k:
                tables(0, k)
            pe.wait_ge(s_bev, 2 * CHUNKS)
            pe.wait_ge(s_am, 2 * CHUNKS)
            transposes(0, 0)
            for l in range(LAYERS):
                for u in range(UNROLL):
                    edge_step(l, 0, u, first=u == 0)
                with pe.Fori(1, GROUPS // UNROLL, 1) as i:
                    for u in range(UNROLL):
                        edge_step(l, i, u)
                sum_messages(l, (l + 1) * GROUPS - 1, 1, UNROLL - 1)
                pe.wait_ge(s_acc, (l + 1) * GROUPS)
                pe.wait_ge(s_hotT, (l + 1) * GROUPS + 1)
                with pe.Fori(0, CHUNKS, 1) as k:
                    kk = l * CHUNKS + k
                    for h in range(2):
                        mm = pe.matmul(PX[:, 0, :], w2[:, l, h, :], agg[:, h, chunk(k)], start=h == 0, stop=h == 1)
                    mm.then_inc(s_z, 1)
                    pe.wait_ge(s_m, kk + 1)
                    for h in range(2):
                        mm = pe.matmul(PX[:, 1 + h, :], v1[:, l, h * P:(h + 1) * P], m_b, start=True, stop=True)
                    mm.then_inc(s_u, 1)
                    if l == 0:
                        pe.matmul(PX[:, 0, :], pw[:, :], hT[:, chunk(k)], start=True, stop=True)
                    pe.wait_ge(s_ur, 2 * kk + 2)
                    if l < LAYERS - 1:
                        for h in range(2):
                            mm = pe.matmul(PX[:, 3, :], v2[:, l, h, :], u_b[:, h, :], start=h == 0, stop=h == 1)
                        mm.then_inc(s_v, 1)
                        tables(l + 1, k)
                    else:
                        for t in range(CT):
                            for h in range(2):
                                mm = pe.matmul(PX[:, 3, t * D:(t + 1) * D], u_b[:, h, t * P:(t + 1) * P],
                                               v2[:, l, h, :], start=h == 0, stop=h == 1)
                        mm.then_inc(s_v, 1)
                        pe.wait_ge(s_y, k + 1)
                if l < LAYERS - 1:
                    pe.wait_ge(s_bev, 2 * CHUNKS * (l + 2))
                    pe.wait_ge(s_am, 2 * CHUNKS * (l + 2))
            with pe.Fori(0, CHUNKS, 1) as k:
                pe.wait_ge(s_x1, k + 1)
                for t in range(CT):
                    mm = pe.transpose(PX[:, 0, t * P:(t + 1) * P], x_b[:, t * D:(t + 1) * D], ident[:, :])
                mm.then_inc(s_x1p, 1)
                pe.wait_ge(s_x1T, k + 1)
                for t in range(CT):
                    mm = pe.matmul(PX[:, 1, t * D:(t + 1) * D], m_b[:, t * P:(t + 1) * P], win2f[:, :],
                                   start=True, stop=True)
                mm.then_inc(s_hf, 1)

            def hidden(g, s, u4, step):
                pe.wait_ge(s_f[u4], (step + 1) * 16)
                if not (isinstance(g, int) and g < 2):
                    pe.wait_ge(s_abs, g - 1)
                    pe.wait_ge(s_q, g - 1)
                pe.matmul(PX[:, s, :], wf1[:, :], fbuf[:, u4, :], start=True, stop=True).then_inc(s_Z, 1)

            pe.wait_ge(s_hs, 3 * CHUNKS)
            pe.wait_ge(s_cnt, NB)
            pe.matmul(PX[:, 0, 0:NB], ones[:, :], many, start=True, stop=True).then_inc(s_tot, 1)
            pe.wait_ge(s_start, 1)
            pe.matmul(PX[:, 1, 0:NB], first_row[:, :], starts, start=True, stop=True, skip_group_check=True)
            pe.matmul(PX[0:NB, 2, 0:1], ends_last, first_row[:, 0:1], start=True, stop=True).then_inc(s_run, 1)
            pe.wait_ge(s_mask, 1)
            for n in range(2):
                mm = pe.matmul(PX[:, 2 + n, 0:SORTED // 2], ones[0:NB, :],
                               M[0:NB, 0, n * (SORTED // 2):(n + 1) * (SORTED // 2)], start=True, stop=True)
            mm.then_inc(s_tb, 1)

            def sort_step(n, s):
                pe.wait_ge(s_ob, n + 1)
                for t in range(STEP):
                    mm = pe.matmul(PX[:, 1, 0:NB], below[:, :], one_bucket[:, s, t, :],
                                   start=False, stop=True, skip_group_check=True)
                mm.then_inc(s_pre, 1)
                pe.wait_ge(s_ps, n + 1)
                for t in range(STEP):
                    mm = pe.matmul(PX[:, 1, 0:NB], not_below[:, :], one_bucket[:, s, t, :],
                                   start=False, stop=True, skip_group_check=True)
                mm.then_inc(s_cum, 1)

            with pe.Fori(0, STEPS // 2, 1) as n:
                for s in range(2):
                    sort_step(n * 2 + s, s)

            def filter_step(i, u):
                g = i * UNROLL + u
                c = LAYERS * GROUPS + g
                if u == UNROLL - 1:
                    hidden(g + 1, 0, 0, i + 1)
                else:
                    hidden(g + 1, (u + 1) % 2, u + 1, i)
                pe.wait_ge(s_hotT, c + 1)
                pe.wait_ge(s_win[u], (LAYERS * (GROUPS // UNROLL) + i + 1) * 16)
                if not (isinstance(g, int) and g < 2):
                    pe.wait_ge(s_xj, g - 1)
                    pe.wait_ge(s_prod, g - 1)
                for j in range(TILES):
                    mm = pe.matmul(PO[:, u % 2, j * D:(j + 1) * D], hotT[:, u % 2, j * P:(j + 1) * P],
                                   A3[:, u, 0:D], start=True, stop=True)
                mm.then_inc(s_X, 1)
                transposes(c + 1, (u + 1) % 2)
                pe.wait_ge(s_sp, g + 1)
                pe.matmul(PX[:, 2 + u % 2, :].rearrange("p (t d) -> p t d", d=D), first_row[:, :],
                          bf2_row[:, :].unsqueeze(1).to_broadcast([P, TILES, D]),
                          start=True, stop=True, skip_group_check=True)
                for j in range(TILES):
                    mm = pe.matmul(PX[:, 2 + u % 2, j * D:(j + 1) * D], sp_b[:, u % 2, j * P:(j + 1) * P],
                                   wf2[:, :], start=False, stop=True, skip_group_check=True)
                mm.then_inc(s_Y, 1)

            hidden(0, 0, 0, 0)
            for u in range(UNROLL):
                filter_step(0, u)
            with pe.Fori(1, GROUPS // UNROLL, 1) as i:
                for u in range(UNROLL):
                    filter_step(i, u)
            pe.wait_ge(s_prod, GROUPS)
            pe.wait_ge(s_abs, GROUPS + 1)
            pe.wait_ge(s_q, GROUPS + 1)

            def sum_sorted(i, u):
                g = i * UNROLL + u
                pe.wait_ge(s_hot128, g + 1)
                if not (isinstance(g, int) and g < 2):
                    pe.wait_ge(s_acc1, (g - 1) * TILES)
                for j in range(TILES):
                    mm = pe.matmul(PX[:, u % 2, j * P:(j + 1) * P], rows[:, u, j, 0:D], hot128[:, u % 2, j, :],
                                   start=True, stop=True)
                mm.then_inc(s_seg1, 1)

            for u in range(UNROLL):
                sum_sorted(0, u)
            with pe.Fori(1, SORTED // TILES // UNROLL, 1) as i:
                for u in range(UNROLL):
                    sum_sorted(i, u)
            pe.wait_ge(s_acc1, SORTED)
            with pe.Fori(0, CHUNKS, 1) as k:
                pe.matmul(PX[:, 0, :], wo1[:, :], agg[:, 0, chunk(k)], start=True, stop=True).then_inc(s_o1, 1)
                pe.wait_ge(s_osp, k + 1)
                for t in range(CT):
                    mm = pe.matmul(PX[:, 3, t * D:(t + 1) * D], sp_b[:, 0, t * P:(t + 1) * P], wo2[:, :],
                                   start=True, stop=True)
                mm.then_inc(s_o2, 1)
                pe.wait_ge(s_y2, k + 1)

        @block.vector
        def _(dve):
            dve.wait_ge(s_w, 16 * (N_W + 1))
            dve.wait_ge(s_tab, 48)
            dve.wait_ge(s_pool0, 14)
            dve.tensor_copy(dst_f[:, :], G[:, 0, 0:TABLE].bitcast(I32)).then_inc(s_c, 1)
            dve.tensor_tensor(out=w1[:, :, 0:H], in0=w1[:, :, 0:H], in1=w1[:, :, H:2 * H],
                              op=ALU.subtract).then_inc(s_c, 1)
            dve.tensor_copy(ident_b[:, :], ident[:, :]).then_inc(s_c, 1)
            dve.tensor_copy(idx[:, :], src_t[:, 0:UNROLL * TILES]).then_inc(s_idx, 2)
            dve.wait_ge(s_bb, 1)
            bases = PX[:, 0, 0:GROUPS + AHEAD]
            dve.tensor_copy(base_i[:, :], bases[0:1, :]).then_inc(s_c, 1)
            dve.tensor_copy(G[:, 1, 0:GROUPS + AHEAD], bases).then_inc(s_c, 1)
            dve.wait_ge(s_c, 5)
            by_tile = dst_f[:, :].rearrange("p (g j) -> p g j", j=TILES)
            dve.tensor_tensor(out=by_tile, in0=by_tile,
                              in1=G[:, 1, 0:GROUPS + AHEAD].unsqueeze(2).to_broadcast([P, GROUPS + AHEAD, TILES]),
                              op=ALU.subtract).then_inc(s_c, 1)
            dve.wait_ge(s_c, 6)

            def split_A(n, k):
                for half in range(2):
                    tt = n * CHUNKS + k
                    q = tt * 2 + half
                    dve.wait_ge(s_tp, q + 1)
                    dve.tensor_tensor(out=Af, in0=tab_bank[half][:, :, 0:H],
                                      in1=b1_bc[:, n:n + 1, :].to_broadcast([P, 2, H]), op=ALU.add).then_inc(s_at, 1)
                    if not (isinstance(q, int) and q < 2):
                        dve.wait_ge(s_store[half], tt * 32)
                    dve.wait_ge(s_at, q * 3 + 1)
                    dve.tensor_copy(A3st[:, half, :, 0, :], Af).then_inc(s_at, 1)
                    dve.wait_ge(s_at, q * 3 + 2)
                    if not (isinstance(q, int) and q < 1):
                        dve.wait_ge(s_lo, q)
                    dve.tensor_tensor(out=Ar, in0=Af, in1=A3st[:, half, :, 0, :], op=ALU.subtract).then_inc(s_at, 1)
                    dve.wait_ge(s_at, q * 3 + 3)
                    dve.tensor_copy(A3st[:, half, :, 1, :], Ar).then_inc(s_am, 1)

            def build_hot(c, g, s, u4, sums=True):
                if not (isinstance(c, int) and c < 2):
                    dve.wait_ge(s_tr, c - 1)
                if sums and not (isinstance(c, int) and c < UNROLL):
                    dve.wait_ge(s_seg, c - UNROLL + 1)
                for j in range(TILES):
                    col = dst_f[:, bass.ds(g * TILES + j, 1)]
                    if sums:
                        dve.tensor_scalar(hot[:, u4, j, :], iota1[:, :], col, None, ALU.is_equal)
                    last = dve.tensor_scalar(hot3[:, s, j, :], iota3[:, :], col, None, ALU.is_equal)
                last.then_inc(s_hot, 1)

            def accumulate(l, c, g, s):
                dve.wait_ge(s_seg, c + 1)
                if not (isinstance(c, int) and c < 1):
                    dve.wait_ge(s_acc, c)
                n = 3 if l == 0 else 2
                b = dve.value_load(base_i[0:1, bass.ds(g, 1)], min_val=0, max_val=NODES)
                window = agg[:, 0:n, bass.ds(b, WIN)]
                dve.tensor_tensor(out=window, in0=window,
                                  in1=PO[:, s, 0:n * WIN].rearrange("p (h w) -> p h w", w=WIN),
                                  op=ALU.add).then_inc(s_acc, 1)

            def stage(g, u):
                dve.tensor_copy(idx[:, (u - 1) * TILES:(u + 1) * TILES],
                                src_t[:, bass.ds((g - 1 + UNROLL) * TILES, 2 * TILES)]).then_inc(s_idx, 1)

            def edge_step(l, i, u, first=False):
                g = i * UNROLL + u
                c = l * GROUPS + g
                build_hot(c + 1, g + 1, (u + 1) % 2, (u + 1) % UNROLL)
                dve.wait_ge(s_G[u], (l * (GROUPS // UNROLL) + i + 1) * TILES * 16)
                dve.wait_ge(s_X, c + 1)
                if not (isinstance(c, int) and c < 2):
                    dve.wait_ge(s_seg, c - 1)
                dve.tensor_tensor(out=M[:, u % 2, :],
                                  in0=PX[:, 2 * (u % 2):2 * (u % 2) + 2, :].rearrange("p b f -> p (b f)"),
                                  in1=G[:, u, :], op=ALU.add).then_inc(s_add, 1)
                if u % 2:
                    stage(g, u)
                if not first:
                    accumulate(l, c - 1, g - 1, (u - 1) % 2)

            def statistics(k, n):
                for t in range(CT):
                    last = dve.bn_stats(st4[:, t, :], y_b[:, t * D:(t + 1) * D])
                last.then_inc(s_bn, 1)
                dve.wait_ge(s_bn, 2 * n + 1)
                dve.tensor_copy(stats[:, bass.ds(k * CT, CT), :], st4[:, :, :])
                dve.tensor_copy(inv[:, chunk(k)], y_b).then_inc(s_bn, 1)
                dve.wait_ge(s_bn, 2 * n + 2)

            def inverse_std(n):
                me, se, mo, so = (stats[:, :, i] for i in (1, 2, 4, 5))
                b = 9 * n
                dve.tensor_tensor(out=mean[:, :], in0=me, in1=mo, op=ALU.add).then_inc(s_nt, 1)
                dve.tensor_tensor(out=veps[:, :], in0=se, in1=so, op=ALU.add).then_inc(s_nt, 1)
                dve.tensor_tensor(out=rstd[:, :], in0=me, in1=mo, op=ALU.subtract).then_inc(s_nt, 1)
                dve.wait_ge(s_nt, b + 3)
                dve.tensor_scalar(mean[:, :], mean[:, :], 0.5, None, ALU.mult)
                dve.tensor_scalar(veps[:, :], veps[:, :], 1.0 / D, EPS, ALU.mult, ALU.add)
                dve.scalar_tensor_tensor(out=std[:, :], in0=rstd[:, :], scalar=0.25, in1=rstd[:, :],
                                         op0=ALU.mult, op1=ALU.mult).then_inc(s_nt, 1)
                dve.wait_ge(s_nt, b + 4)
                dve.tensor_tensor(out=veps[:, :], in0=veps[:, :], in1=std[:, :], op=ALU.add).then_inc(s_var, 1)
                dve.wait_ge(s_var, n + 1)
                dve.wait_ge(s_std, n + 1)
                dve.reciprocal(rstd[:, :], std[:, :]).then_inc(s_nt, 1)
                dve.wait_ge(s_nt, b + 5)
                dve.tensor_tensor(out=rstd[:, :], in0=rstd[:, :], in1=veps[:, :], op=ALU.mult).then_inc(s_nt, 1)
                dve.wait_ge(s_nt, b + 6)
                dve.tensor_tensor(out=rstd[:, :], in0=rstd[:, :], in1=std[:, :], op=ALU.add).then_inc(s_nt, 1)
                dve.wait_ge(s_nt, b + 7)
                dve.tensor_scalar(rstd[:, :], rstd[:, :], 0.5, None, ALU.mult).then_inc(s_nt, 1)
                dve.wait_ge(s_nt, b + 8)
                dve.reciprocal(rstd[:, :], rstd[:, :]).then_inc(s_nt, 1)
                dve.wait_ge(s_nt, b + 9)

            def normalise(k, tiles):
                for t in range(tiles):
                    row = inv[:, bass.ds((k * CT + t) * D, D)]
                    last = dve.tensor_scalar(row, row, mean[:, bass.ds(k * CT + t, 1)],
                                             rstd[:, bass.ds(k * CT + t, 1)], ALU.subtract, ALU.mult)
                return last

            dve.tensor_copy(h_b, hT[:, 0:CHUNK]).then_inc(s_h, 1)
            split_A(0, 0)
            with dve.Fori(1, CHUNKS, 1) as k:
                dve.wait_ge(s_tp, 2 * k)
                dve.tensor_copy(h_b, hT[:, chunk(k)]).then_inc(s_h, 1)
                split_A(0, k)
            build_hot(0, 0, 0, 0)
            for l in range(LAYERS):
                dve.wait_ge(s_zero, 1 + 2 * l * CHUNKS)
                for half in range(2):
                    dve.wait_ge(s_store[half], (l + 1) * CHUNKS * 32)
                for u in range(UNROLL):
                    edge_step(l, 0, u, first=u == 0)
                with dve.Fori(1, GROUPS // UNROLL, 1) as i:
                    for u in range(UNROLL):
                        edge_step(l, i, u)
                accumulate(l, (l + 1) * GROUPS - 1, GROUPS - 1, 1)
                if l == 0:
                    dve.wait_ge(s_acc, GROUPS)
                    dve.tensor_scalar(inv[:, :], agg[:, 2, :], 1.0, None, ALU.max).then_inc(s_t, 1)
                    dve.wait_ge(s_t, 1)
                    dve.reciprocal(inv[:, :], inv[:, :]).then_inc(s_t, 1)
                    dve.wait_ge(s_t, 2)
                with dve.Fori(0, CHUNKS, 1) as k:
                    kk = l * CHUNKS + k
                    st = 2 + 2 * kk
                    dve.wait_ge(s_z, kk + 1)
                    dve.scalar_tensor_tensor(out=t_b, in0=agg[:, 2, chunk(k)], scalar=b2_col[:, l:l + 1],
                                             in1=PX[:, 0, :], op0=ALU.mult, op1=ALU.add).then_inc(s_t, 1)
                    dve.wait_ge(s_t, st + 1)
                    dve.tensor_tensor(out=m_b, in0=t_b, in1=inv[:, chunk(k)], op=ALU.mult).then_inc(s_m, 1)
                    dve.wait_ge(s_v, kk + 1)
                    if l < LAYERS - 1:
                        dve.tensor_scalar(r_b, PX[:, 3, :], c2_col[:, l:l + 1], 0.0, ALU.add, ALU.max).then_inc(s_t, 1)
                        dve.wait_ge(s_t, st + 2)
                        if l == 0:
                            dve.scalar_tensor_tensor(out=h_b, in0=PX[:, 0, :], scalar=pb_col[:, 0:1],
                                                     in1=r_b, op0=ALU.add, op1=ALU.add).then_inc(s_h, 1)
                        else:
                            dve.wait_ge(s_keep, CHUNKS)
                            dve.tensor_tensor(out=h_b, in0=hT[:, chunk(k)], in1=r_b,
                                              op=ALU.add).then_inc(s_h, 1)
                        split_A(l + 1, k)
                    else:
                        dve.wait_ge(s_xres, 16 * (k + 1))
                        yb = r_b.rearrange("p (t d) -> p t d", d=D)
                        dve.tensor_tensor(out=yb, in0=PX[:, 3, :].rearrange("p (t d) -> p t d", d=D),
                                          in1=c2_bc[:, :].unsqueeze(1).to_broadcast([P, CT, D]),
                                          op=ALU.add).then_inc(s_t, 1)
                        dve.wait_ge(s_t, st + 2)
                        dve.tensor_tensor(out=y_b.rearrange("p (t d) -> p t d", d=D), in0=yb, in1=xres.rearrange("p (t d) -> p t d", d=D),
                                          op=ALU.add).then_inc(s_y, 1)
                        dve.wait_ge(s_y, k + 1)
                        statistics(k, k)
            inverse_std(0)
            with dve.Fori(0, CHUNKS, 1) as k:
                normalise(k, CT).then_inc(s_nx, 1)
                dve.wait_ge(s_nx, k + 1)
                dve.tensor_copy(x_b, inv[:, chunk(k)]).then_inc(s_x1, 1)
                hf = PX[:, 1, :].rearrange("p (t d) -> p t d", d=D)
                dve.wait_ge(s_hf, k + 1)
                dve.wait_ge(s_xres, (CHUNKS + k) * 16)
                dve.tensor_copy(H3st[:, :, 0, :], hf).then_inc(s_hs, 1)
                dve.wait_ge(s_hs, 3 * k + 1)
                dve.tensor_tensor(out=xres_t, in0=hf, in1=H3st[:, :, 0, :], op=ALU.subtract).then_inc(s_hs, 1)
                dve.wait_ge(s_hs, 3 * k + 2)
                dve.tensor_copy(H3st[:, :, 1, :], xres_t).then_inc(s_hs, 1)

            def shifted_softplus(c, s):
                dve.wait_ge(s_abs, c + 1)
                if not (isinstance(c, int) and c < 1):
                    dve.wait_ge(s_sp, c)
                dve.tensor_scalar(q_b, PX[:, s, :], bf1_col[:, 0:1], 0.0, ALU.add, ALU.max).then_inc(s_q, 1)
                dve.wait_ge(s_q, c + 1)
                dve.wait_ge(s_ln, c + 1)
                if not (isinstance(c, int) and c < 2):
                    dve.wait_ge(s_Y, c - 1)
                dve.scalar_tensor_tensor(out=sp_b[:, s, :], in0=q_b, scalar=-LOG2, in1=l_b,
                                         op0=ALU.add, op1=ALU.add).then_inc(s_sp, 1)

            steps = [0]

            def after(ins):
                steps[0] += 1
                ins.then_inc(s_rt, 1)
                dve.wait_ge(s_rt, steps[0])

            source = src_t[:, 0:GROUPS * TILES]
            dve.wait_ge(s_hlo, CHUNKS)
            after(dve.tensor_scalar(place_i, source, 7, None, ALU.arith_shift_right))
            after(dve.tensor_copy(bucket_f, place_i))
            after(dve.scalar_tensor_tensor(out=loc_f, in0=bucket_f, scalar=-float(P), in1=source,
                                           op0=ALU.mult, op1=ALU.add))
            for b in range(NB):
                dve.tensor_scalar(place_f, bucket_f, float(b), 0.0, ALU.is_equal, ALU.add,
                                  accum_out=many[:, b:b + 1]).then_inc(s_cnt, 1)
                dve.wait_ge(s_cnt, b + 1)
            dve.wait_ge(s_tot, 1)
            after(dve.tensor_scalar(tiles_i, PX[:, 0, 0:NB], float(P - 1), None, ALU.add))
            after(dve.tensor_scalar(tiles_i, tiles_i, 7, None, ALU.arith_shift_right))
            after(dve.tensor_copy(tiles_b, tiles_i))
            summed, d, pair = tiles_b, 1, [ends, ends2]
            while d < NB:
                dve.tensor_copy(pair[0][:, 0:d], summed[:, 0:d])
                after(dve.tensor_tensor(out=pair[0][:, d:NB], in0=summed[:, d:NB], in1=summed[:, 0:NB - d], op=ALU.add))
                summed, d, pair = pair[0], 2 * d, pair[::-1]
            assert summed is ends_last
            after(dve.tensor_tensor(out=starts, in0=summed, in1=tiles_b, op=ALU.subtract))
            after(dve.tensor_scalar(starts, starts, float(P), None, ALU.mult))
            dve.tensor_scalar(full, tiles_b, 1.0, None, ALU.min).then_inc(s_start, 1)
            dve.wait_ge(s_start, 1)
            head = zero_list_f[:, 0:NB]
            dve.wait_ge(s_zero, 3 + (2 * LAYERS - 1) * CHUNKS)
            after(dve.scalar_tensor_tensor(out=head, in0=summed, scalar=-float(SPARE + 1), in1=iota_b[:, :],
                                           op0=ALU.add, op1=ALU.subtract))
            after(dve.tensor_tensor(out=head, in0=head, in1=full, op=ALU.mult))
            after(dve.scalar_tensor_tensor(out=head, in0=head, scalar=float(SPARE), in1=iota_b[:, :],
                                           op0=ALU.add, op1=ALU.add))
            after(dve.tensor_scalar(zero_list_f[:, NB:NB + TAIL], iota_t[:, 0:TAIL], summed[:, NB - 1:NB],
                                    None, ALU.add))
            dve.tensor_copy(zero_list[0:1, :], zero_list_f[0:1, :]).then_inc(s_list, 1)
            dve.wait_ge(s_run, 1)
            after(dve.tensor_copy(col_end[0:NB, :], PX[0:NB, 2, 0:1]))
            dve.tensor_scalar(M[0:NB, 0, 0:SORTED], iota_t[0:NB, :], col_end[0:NB, :], None,
                              ALU.is_ge).then_inc(s_mask, 1)
            dve.wait_ge(s_tb, 1)
            for n in range(2):
                after(dve.tensor_scalar(node_base[0:1, n * (SORTED // 2):(n + 1) * (SORTED // 2)],
                                        PX[0:1, 2 + n, 0:SORTED // 2], float(P), None, ALU.mult))

            by_step = bucket_f.rearrange("p (s t) -> p s t", t=STEP)
            earlier = M[:, 1, 0:GROUPS * TILES]
            earlier_s = earlier.rearrange("p (s t) -> p s t", t=STEP)
            after(dve.memset(earlier, 0.0))
            for d in range(1, STEP):
                same = M[:, 0, 0:STEPS * (STEP - d)].rearrange("p (s t) -> p s t", t=STEP - d)
                after(dve.tensor_tensor(out=same, in0=by_step[:, :, d:STEP], in1=by_step[:, :, 0:STEP - d],
                                        op=ALU.is_equal))
                after(dve.tensor_tensor(out=earlier_s[:, :, d:STEP], in0=earlier_s[:, :, d:STEP], in1=same,
                                        op=ALU.add))

            def build_buckets(n, s):
                if not (isinstance(n, int) and n < 2):
                    dve.wait_ge(s_cum, n - 1)
                dve.tensor_tensor(
                    out=one_bucket[:, s, :, :],
                    in0=bucket_f[:, bass.ds(n * STEP, STEP)].unsqueeze(2).to_broadcast([P, STEP, NB]),
                    in1=iota_b[:, :].unsqueeze(1).to_broadcast([P, STEP, NB]),
                    op=ALU.is_equal).then_inc(s_ob, 1)

            def pick_places(n, s, more=True):
                dve.wait_ge(s_pre, n + 1)
                if not (isinstance(n, int) and n < 1):
                    dve.wait_ge(s_pick, n)
                dve.tensor_tensor(out=picked, in0=one_bucket[:, s, :, :],
                                  in1=PX[:, 1, 0:NB].unsqueeze(1).to_broadcast([P, STEP, NB]),
                                  op=ALU.mult).then_inc(s_ps, 1)
                dve.wait_ge(s_ps, n + 1)
                if more:
                    build_buckets(n + 1, 1 - s)
                dve.tensor_reduce(out=place_f[:, bass.ds(n * STEP, STEP)], in_=picked, axis=mybir.AxisListType.X,
                                  op=ALU.add).then_inc(s_pick, 1)

            build_buckets(0, 0)
            pick_places(0, 0)
            pick_places(1, 1)
            with dve.Fori(1, STEPS // 2 - 1, 1) as n:
                for s in range(2):
                    pick_places(n * 2 + s, s)
            pick_places(STEPS - 2, 0)
            pick_places(STEPS - 1, 1, more=False)
            dve.wait_ge(s_pick, STEPS)
            dve.wait_ge(s_cum, STEPS)
            dve.tensor_tensor(out=place_i, in0=place_f, in1=earlier, op=ALU.add).then_inc(s_place, 1)

            def filter_step(i, u):
                g = i * UNROLL + u
                c = LAYERS * GROUPS + g
                landed = (LAYERS * (GROUPS // UNROLL) + i) * TILES * 16
                if u % 2 == 0:
                    dve.wait_ge(s_G[u], landed)
                    dve.wait_ge(s_G[u + 1], landed)
                    dve.tensor_copy(idx[:, u * TILES:(u + 2) * TILES],
                                    place_i[:, bass.ds(g * TILES, 2 * TILES)]).then_inc(s_idx, 1)
                build_hot(c + 1, g + 1, (u + 1) % 2, 0, sums=False)
                dve.wait_ge(s_xj, g + 1)
                dve.wait_ge(s_Y, g + 1)
                for j in range(TILES):
                    t = bass.ds(g * TILES + j, 1)
                    dve.scalar_tensor_tensor(out=rows[:, u, j, 0:D], in0=xj_b[:, u % 2, j * D:(j + 1) * D],
                                             scalar=rcut_t[:, t], in1=PX[:, 2 + u % 2, j * D:(j + 1) * D],
                                             op0=ALU.mult, op1=ALU.mult)
                dve.tensor_copy(rows[:, u, :, D], loc_f[:, bass.ds(g * TILES, TILES)]).then_inc(s_prod, 1)
                shifted_softplus(g + 1, (u + 1) % 2)

            dve.wait_ge(s_rcut, 16)
            dve.wait_ge(s_place, 1)
            shifted_softplus(0, 0)
            for u in range(UNROLL):
                filter_step(0, u)
            with dve.Fori(1, GROUPS // UNROLL, 1) as i:
                for u in range(UNROLL):
                    filter_step(i, u)

            def sorted_step(i, u, first=False):
                g = i * UNROLL + u
                dve.wait_ge(s_row[u], 16 * (i + 1))
                if not (isinstance(g, int) and g < 2):
                    dve.wait_ge(s_seg1, g - 1)
                for j in range(TILES):
                    last = dve.tensor_scalar(hot128[:, u % 2, j, :], iota_t[:, 0:P], rows[:, u, j, D:ROW], None,
                                             ALU.is_equal)
                last.then_inc(s_hot128, 1)
                if not first:
                    add_sorted(g - 1, (u - 1) % 2)

            def add_sorted(g, s):
                dve.wait_ge(s_seg1, g + 1)
                for j in range(TILES):
                    t = g * TILES + j
                    if not (isinstance(t, int) and t < 1):
                        dve.wait_ge(s_acc1, t)
                    b = dve.value_load(node_base[0:1, bass.ds(t, 1)], min_val=0, max_val=NB * P)
                    window = agg[:, 0, bass.ds(b, P)]
                    dve.tensor_tensor(out=window, in0=window, in1=PX[:, s, j * P:(j + 1) * P],
                                      op=ALU.add).then_inc(s_acc1, 1)

            for u in range(UNROLL):
                sorted_step(0, u, first=u == 0)
            with dve.Fori(1, SORTED // TILES // UNROLL, 1) as i:
                for u in range(UNROLL):
                    sorted_step(i, u)
            add_sorted(SORTED // TILES - 1, 1)
            with dve.Fori(0, CHUNKS, 1) as k:
                dve.wait_ge(s_oa, 3 * k + 1)
                dve.tensor_scalar(r_b, PX[:, 0, :], bo1_col[:, 0:1], 0.0, ALU.add, ALU.max).then_inc(s_ot, 1)
                dve.wait_ge(s_ot, 2 * k + 1)
                dve.wait_ge(s_oa, 3 * k + 3)
                dve.scalar_tensor_tensor(out=sp_b[:, 0, :], in0=r_b, scalar=-LOG2, in1=xres,
                                         op0=ALU.add, op1=ALU.add).then_inc(s_osp, 1)
                dve.wait_ge(s_o2, k + 1)
                yk = y_b.rearrange("p (t d) -> p t d", d=D)
                dve.tensor_tensor(out=y_b, in0=inv[:, chunk(k)], in1=PX[:, 3, :], op=ALU.add).then_inc(s_ot, 1)
                dve.wait_ge(s_ot, 2 * k + 2)
                dve.tensor_tensor(out=yk, in0=yk, in1=bo2_bc[:, :].unsqueeze(1).to_broadcast([P, CT, D]),
                                  op=ALU.add).then_inc(s_y2, 1)
                dve.wait_ge(s_y2, k + 1)
                statistics(k, CHUNKS + k)
            inverse_std(1)
            with dve.Fori(0, FULL_TILES // CT, 1) as k:
                normalise(k, CT).then_inc(s_norm, 1)
            normalise(FULL_TILES // CT, 1).then_inc(s_norm, 1)


def kernel(**inputs):
    import numpy as _np
    import concourse.bacc as _bacc
    from concourse import mybir as _mybir
    from concourse.bass_utils import run_bass_kernel_spmd as _run

    a = {n: _np.ascontiguousarray(v) for n, v in inputs.items()}

    def edge_table(v, pad):
        whole = _np.full(GROUPS * GROUP, pad, v.dtype)
        whole[:EDGES] = v
        t = whole.reshape(GROUPS * TILES, P).T
        return _np.ascontiguousarray(_np.concatenate([t, t[:, :AHEAD * TILES]], axis=1))

    xN = _np.zeros((NPAD, D), a["x"].dtype)
    xN[:NODES] = a["x"]
    fT = _np.zeros((RBF, (GROUPS + 1) * GROUP), a["edge_attr_20"].dtype)
    fT[:, :EDGES] = a["edge_attr_20"].T
    c0 = lambda v: _np.ascontiguousarray(v)
    laid = {
        "xT": c0(xN.T), "xN": xN,
        "src": edge_table(a["src"], 0), "dst": edge_table(a["dst"], -1),
        "rcut": edge_table(a["edge_weight"], 0), "fT": fT,
        "phi_w1": a["L0_gnn_phi_w1"], "phi_b1": a["L0_gnn_phi_b1"], "phi_w2": a["L0_gnn_phi_w2"],
        "phi_b2": c0(a["L0_gnn_phi_b2"].T), "psi_w1": a["L0_gnn_psi_w1"],
        "psi_b1": c0(a["L0_gnn_psi_b1"].reshape(LAYERS, 2, P).transpose(2, 0, 1)),
        "psi_w2": a["L0_gnn_psi_w2"], "psi_b2": c0(a["L0_gnn_psi_b2"].T),
        "psi_b2_last": c0(a["L0_gnn_psi_b2"][LAYERS - 1:]),
        "proj_w": a["L0_gnn_proj_w"], "proj_b": a["L0_gnn_proj_b"].reshape(P, 1),
        "w_in2f": a["L1_gnn_W_in2f"], "w_f1": a["L1_gnn_W_f1"], "b_f1": a["L1_gnn_b_f1"].reshape(P, 1),
        "w_f2": a["L1_gnn_W_f2"], "b_f2": a["L1_gnn_b_f2"].reshape(1, D),
        "w_o1": a["L1_gnn_W_o1"], "b_o1": a["L1_gnn_b_o1"].reshape(P, 1),
        "w_o2": a["L1_gnn_W_o2"], "b_o2": a["L1_gnn_b_o2"].reshape(1, D),
    }
    nc = _bacc.Bacc("TRN2", target_bir_lowering=False, num_devices=1)
    arrays, args = {}, {}
    for name, v in laid.items():
        arrays[f"in_{name}"] = v
        args[name] = nc.dram_tensor(f"in_{name}", v.shape, _mybir.dt.from_np(v.dtype), kind="ExternalInput").ap()
    args["out"] = nc.dram_tensor("out_0", (NODES, D), _mybir.dt.float32, kind="ExternalOutput").ap()
    build(nc, **args)
    r = _run(nc, [arrays], core_ids=[0])
    return r.results[0]["out_0"]
```

```python
import numpy as np
import concourse.bass as bass
from concourse import mybir
from contextlib import ExitStack

F32 = mybir.dt.float32
BF16 = mybir.dt.bfloat16
I32 = mybir.dt.int32
ALU = mybir.AluOpType
ACT = mybir.ActivationFunctionType

P = 128
NODES, EDGES, D, H, RBF, LAYERS = 6250, 106250, 128, 256, 20, 3
TILES = 4
GROUP = TILES * P
UNROLL = 4
GROUPS = -(-EDGES // (GROUP * UNROLL)) * UNROLL
AHEAD = 4
TABLE = (GROUPS + AHEAD) * TILES
WIN = 42
WIN3 = 3 * WIN
CHUNK = 512
CHUNKS = -(-NODES // CHUNK)
NPAD = CHUNK * CHUNKS
CT = CHUNK // P
NB = -(-NODES // P)
STEP = 8
STEPS = GROUPS * TILES // STEP
CLEARS = STEPS
TAIL = CLEARS - NB
PER_CHUNK = STEPS // CHUNKS
SLOTS = 6
SORTED = -(-(GROUPS + NB) // SLOTS) * SLOTS
assert CLEARS >= NB + SORTED - GROUPS
SPARE = SORTED + NB
ROW = D + 1
LOG2 = float(np.log(2.0))
EPS = 1e-5
EDGE_TILES = GROUPS * TILES
FULL_TILES, REST = NODES // P, NODES % P


def build(nc, xT, xN, src, dst, rcut, fT, phi_w1, phi_b1, phi_w2, phi_b2, psi_w1, psi_b1, psi_w2,
          psi_b2, psi_b2_last, proj_w, proj_b, w_in2f, w_f1, b_f1, w_f2, b_f2, w_o1, b_o1, w_o2, b_o2, out):
    ctx = ExitStack()
    with ctx:
        def sb(name, shape, dt=F32):
            return ctx.enter_context(nc.sbuf_tensor(name, shape, dt))

        def ps(name, shape, dt=F32):
            return ctx.enter_context(nc.psum_tensor(name, shape, dt))

        def sem(name):
            return ctx.enter_context(nc.semaphore(name))

        B_d = [nc.dram_tensor(f"B_table{l}", [NPAD, H], F32, kind="Internal").ap() for l in range(LAYERS)]
        A3_d = [nc.dram_tensor(f"A_table{l}", [NPAD * 3, H], BF16, kind="Internal").ap() for l in range(LAYERS)]
        hf3_d = nc.dram_tensor("filter_table", [NPAD * 3, D], BF16, kind="Internal").ap()
        hf_edge_d = nc.dram_tensor("filter_rows_by_edge", [EDGE_TILES * P, D], F32, kind="Internal").ap()
        sorted_d = nc.dram_tensor("sorted_messages", [(SPARE + NB) * GROUP, ROW], F32, kind="Internal").ap()

        w1 = sb("w1", [P, LAYERS, 2 * H])
        w2 = sb("w2", [P, LAYERS, 2, D])
        v1 = sb("v1", [P, LAYERS, H])
        v2 = sb("v2", [P, LAYERS, 2, D])
        b1_bc = sb("b1_bc", [P, LAYERS, H])
        b2_col = sb("b2_col", [P, LAYERS])
        c1_col = sb("c1_col", [P, LAYERS, 2])
        c2_col = sb("c2_col", [P, LAYERS])
        c2_bc = sb("c2_bc", [P, D])
        pw = sb("pw", [P, D])
        pb_col = sb("pb_col", [P, 1])
        win2f = sb("win2f", [P, D])
        wf1 = sb("wf1", [RBF, D])
        wf2 = sb("wf2", [P, D])
        wo1 = sb("wo1", [P, D])
        wo2 = sb("wo2", [P, D])
        bf1_col = sb("bf1_col", [P, 1])
        bo1_col = sb("bo1_col", [P, 1])
        bo2_bc = sb("bo2_bc", [P, D])
        bf2_row = sb("bf2_row", [P, D])
        bf2_3 = sb("bf2_3", [P, D], BF16)
        first_row = sb("first_row", [P, P])
        ones = sb("ones", [P, P])
        ones_b = sb("ones_b", [P, P], BF16)
        ident_b = sb("ident_b", [P, P], BF16)
        ident = sb("ident", [P, P])
        iota3 = sb("iota3", [P, WIN3], BF16)
        iota1 = sb("iota1", [P, WIN])

        src_t = sb("src_t", [P, TABLE], I32)
        dst_f = sb("dst_f", [P, TABLE])
        base_i = sb("base_i", [1, GROUPS + AHEAD], I32)

        outside = sb("outside", [P, 1])
        outside_i = sb("outside_i", [P, 1], I32)
        far_i = sb("far_i", [P, 3], I32)
        far_f = sb("far_f", [P, 4])

        iota_b = sb("iota_b", [P, NB])
        below = sb("below", [P, P], BF16)
        not_below = sb("not_below", [P, P], BF16)
        idx = sb("idx", [P, UNROLL * TILES], I32)
        G = sb("G", [P, UNROLL, TILES * H])
        A3 = sb("A3", [WIN3, UNROLL, H], BF16)
        hot3 = sb("hot3", [P, 2, TILES, WIN3], BF16)
        hotT = sb("hotT", [WIN3, 2, GROUP], BF16)
        hot = sb("hot", [P, UNROLL, TILES, WIN])
        M = sb("M", [P, 2, TILES * H])
        S = sb("S", [P, 3, P])
        agg = sb("agg", [P, 3, NPAD])
        inv = sb("inv", [P, NPAD])
        hT = sb("hT", [P, NPAD])
        st4 = sb("st4", [P, CT, 6])
        stats = sb("stats", [P, CHUNKS * CT, 6])
        mean = sb("mean", [P, CHUNKS * CT])
        zeros = sb("zeros", [P, 1])
        veps = sb("veps", [P, CHUNKS * CT])
        std = sb("std", [P, CHUNKS * CT])
        rstd = sb("rstd", [P, CHUNKS * CT])
        x1 = inv[:, :].rearrange("p (t d) -> p t d", d=D)
        m_b = G[:, 0, 0:CHUNK]
        t_b = G[:, 0, CHUNK:2 * CHUNK]
        u_b = G[:, 1, :].rearrange("p (h n) -> p h n", h=2)
        r_b = G[:, 2, 0:CHUNK]
        xres = G[:, 2, CHUNK:2 * CHUNK]
        h_b = G[:, 3, 0:CHUNK]
        x_b = G[:, 3, CHUNK:2 * CHUNK]
        xres_t = xres.rearrange("p (t d) -> p t d", d=D)
        Bst = M[:, :, 0:2 * H].rearrange("p s (t f) -> p s t f", t=2)
        Af = M[:, 0, 2 * H:4 * H].rearrange("p (t f) -> p t f", t=2)
        Ar = M[:, 1, 2 * H:4 * H].rearrange("p (t f) -> p t f", t=2)
        A3st = sb("A3st", [P, 2, 2, 3, H], BF16)
        H3st = A3st[:, 0, :, :, :].rearrange("p t c f -> p (t c f)").rearrange(
            "p (t c f) -> p t c f", t=CT, c=3)
        y_b = x_b
        far_B = G[:, 0, 0:H]
        far_A3 = G[:, 1, 0:3 * H // 2].bitcast(BF16).rearrange("p (c f) -> p c f", c=3)
        far_hf3 = G[:, 1, 0:3 * D // 2].bitcast(BF16).rearrange("p (c f) -> p c f", c=3)
        far_hot = G[:, 2, 0:CHUNK]
        far_iota = G[:, 3, 0:CHUNK]
        far_m = M[:, 0, 0:H]
        far_hf = M[:, 0, 0:D]
        zone = agg[:, 1:3, :].rearrange("p a n -> p (a n)")
        taken = [0]

        def part(n, dt=F32):
            at = taken[0]
            taken[0] += n
            assert taken[0] <= 2 * NPAD
            words = zone[:, at:at + n]
            return words if dt == F32 else words.bitcast(dt)

        bucket_f = part(GROUPS * TILES)
        bucket_b = part(GROUPS * TILES // 2).bitcast(BF16)
        iota_bb = part(NB).bitcast(BF16)[:, 0:NB]
        place_f = part(GROUPS * TILES)
        one_bucket = part(2 * STEP * NB).bitcast(BF16).rearrange("p (s t b) -> p s t b", s=4, t=STEP)
        prefix = part(2 * NB).rearrange("p (s b) -> p s b", s=2)
        picked = part(2 * STEP * NB).rearrange("p (s t b) -> p s t b", s=2, b=NB)
        many = part(NB)
        groups_b, ends, ends2, starts, full = part(NB), part(NB), part(NB), part(NB), part(NB)
        groups_i = part(NB, I32)
        zero_list_f = part(CLEARS)
        col_end = part(1)
        taken[0] = 0
        fbuf = part(UNROLL * GROUP)[0:RBF, :].rearrange("p (s e) -> p s e", s=UNROLL)
        a_b, e_b, l_b, q_b = part(GROUP), part(GROUP), part(GROUP), part(GROUP)
        sp_b = part(2 * GROUP).rearrange("p (s e) -> p s e", s=2)
        xj_b = part(2 * GROUP).rearrange("p (s e) -> p s e", s=2)
        xj_far = part(GROUP)
        rcut_t = part(TABLE)
        loc_f = part(GROUPS * TILES)
        place_i = part(GROUPS * TILES, I32)
        iota_t = part(SORTED)
        zero_rows = part(ROW)
        zero_list = part(CLEARS, I32)
        node_base = part(SORTED, I32)
        ends_last = [ends, ends2][(NB - 1).bit_length() % 2 - 1]
        rows = G[:, :, 0:TILES * ROW].rearrange("p u (t w) -> p u t w", w=ROW)
        sorted_rows = G[:, :, :].rearrange("p u w -> p (u w)")[:, 0:SLOTS * TILES * ROW].rearrange(
            "p (u t w) -> p u t w", u=SLOTS, w=ROW)
        hot128 = M[:, :, 0:TILES * P].rearrange("p s (t n) -> p s t n", n=P)

        PX = ps("PX", [P, 4, 512])
        PO = ps("PO", [P, 2, 512])
        PT = ps("PT", [P, 2, 512])
        PTb = [PT[:, s, :].bitcast(BF16) for s in range(2)]
        tab_bank = [PO, PT]

        s_w = sem("weights_in")
        s_tab = sem("edge_tables_in")
        s_pool0 = sem("pool_constants")
        s_c = sem("vector_constants")
        s_bb = sem("bases_spread")
        s_bf2 = sem("bias_split_step")
        s_os = sem("outside_step")
        s_osum = sem("outside_summed")
        s_far_dst = sem("far_dst_in")
        s_far_idx = sem("far_indices")
        s_far_rows = [sem(f"far_rows_gathered{l}") for l in range(LAYERS + 1)]
        s_far_step = sem("far_message_step")
        s_far_hot = sem("far_hot_built")
        s_far_seg = sem("far_summed")
        s_far_acc = sem("far_added")
        s_far_iota = sem("far_iota")
        s_far_hf = sem("far_filter_rows")
        s_far_out = sem("far_filter_rows_out")
        s_far_xj = sem("far_rows_back")
        s_idx = sem("indices_staged")
        s_G = [sem(f"rows_gathered{i}") for i in range(UNROLL)]
        s_win = [sem(f"window_in{i}") for i in range(UNROLL)]
        s_hot = sem("hot_built")
        s_tr = sem("hot_transposed")
        s_hotT = sem("hotT_ready")
        s_X = sem("A_spread")
        s_add = sem("pre_relu_ready")
        s_M = sem("messages_ready")
        s_seg = sem("messages_summed")
        s_S = sem("sums_copied")
        s_back = sem("sums_transposed")
        s_acc = sem("agg_added")
        s_zero = sem("agg_zeroed")
        s_z = sem("z_ready")
        s_t = sem("vector_step")
        s_m = sem("mean_ready")
        s_u = sem("u_ready")
        s_ur = sem("u_relu")
        s_v = sem("v_ready")
        s_x0 = sem("x_chunk_copied")
        s_r = sem("psi_relu_ready")
        s_inv = sem("inverse_counts")
        s_pr = sem("residual_projected")
        s_prc = sem("projection_copied")
        s_h = sem("h_ready")
        s_tp = sem("table_product")
        s_bev = sem("B_rows_copied")
        s_at = sem("A_split_step")
        s_am = sem("A_two_parts")
        s_lo = sem("A_third_part")
        s_store = [sem(f"table_stored{i}") for i in range(2)]
        s_xres = sem("x_rows_in")
        s_y = sem("y_ready")
        s_var = sem("variances_ready")
        s_std = sem("std_ready")
        s_x1 = sem("x1_ready")
        s_x1p = sem("x1_transposed")
        s_x1T = sem("x1T_copied")
        s_keep = sem("features_kept")
        s_nx = sem("x1_normed")
        s_bn = sem("statistics_step")
        s_nt = sem("newton_step")
        s_ot = sem("output_vector_step")
        s_hf = sem("hf_product")
        s_hs = sem("hf_split_step")
        s_hlo = sem("hf_third_part")
        s_rcut = sem("rcut_in")
        s_rt = sem("route_step")
        s_cnt = sem("bucket_counted")
        s_tot = sem("bucket_totals")
        s_start = sem("bucket_starts")
        s_run = sem("running_starts")
        s_mask = sem("group_masks")
        s_tb = sem("group_buckets")
        s_list = sem("lists_ready")
        s_ob = sem("bucket_hot_built")
        s_pre = sem("prefix_added")
        s_ps = sem("prefix_copied")
        s_mul = sem("prefix_masked")
        s_pick = sem("places_picked")
        s_cum = sem("step_added")
        s_clear = sem("gaps_cleared")
        s_place = sem("places_ready")
        s_f = [sem(f"f_in{i}") for i in range(UNROLL)]
        s_Z = sem("filter_hidden")
        s_abs = sem("abs_ready")
        s_exp = sem("exp_ready")
        s_ln = sem("ln_ready")
        s_q = sem("q_ready")
        s_sp = sem("softplus_ready")
        s_Y = sem("filter_ready")
        s_xj = sem("rows_by_edge_copied")
        s_prod = sem("x_ij_ready")
        s_row = [sem(f"sorted_in{i}") for i in range(SLOTS)]
        s_hot128 = sem("bucket_nodes_hot")
        s_seg1 = sem("x_ij_summed")
        s_acc1 = sem("agg1_added")
        s_o1 = sem("o1_ready")
        s_oa = sem("o_act_step")
        s_osp = sem("o_softplus")
        s_o2 = sem("o2_ready")
        s_oy = sem("residual_added")
        s_y2 = sem("y2_ready")
        s_norm = sem("rows_normed")
        s_out = sem("rows_out")

        N_W = 24

        block = ctx.enter_context(nc.Block())

        def any_outside(eng):
            eng.wait_ge(s_os, 6)
            return eng.value_load(outside_i[0:1, 0:1], min_val=0, max_val=P * TABLE) > 0
        chunk = lambda k: bass.ds(k * CHUNK, CHUNK)

        @block.sync
        def _(sp):
            sp.dma_start(src_t[:, :], src).then_inc(s_tab, 16)
            sp.dma_start(G[:, 0, 0:TABLE].bitcast(I32), dst).then_inc(s_tab, 16)
            sp.dma_start(hT[:, :], xT).then_inc(s_tab, 16)
            loads = [
                (w1[:, :, 0:H], phi_w1[:, 0:P, :].rearrange("l p f -> p l f")),
                (w1[:, :, H:2 * H], phi_w1[:, P:2 * P, :].rearrange("l p f -> p l f")),
                (b1_bc[:, :, :], phi_b1.rearrange("(a l) f -> a l f", a=1).to_broadcast([P, LAYERS, H])),
                (v1[:, :, :], psi_w1.rearrange("l p f -> p l f")),
                (b2_col[:, :], phi_b2), (c2_col[:, :], psi_b2),
                (c1_col[:, :, :], psi_b1),
                (pw[:, :], proj_w), (pb_col[:, :], proj_b),
                (win2f[:, :], w_in2f), (wf1[:, :], w_f1), (wf2[:, :], w_f2),
                (wo1[:, :], w_o1), (wo2[:, :], w_o2), (bf1_col[:, :], b_f1), (bo1_col[:, :], b_o1),
                (bo2_bc[:, :], b_o2.to_broadcast([P, D])),
                (c2_bc[:, :], psi_b2_last.to_broadcast([P, D])),
            ]
            for l in range(LAYERS):
                loads.append((w2[:, l, :, :], phi_w2[l].rearrange("(h p) d -> p h d", p=P)))
                loads.append((v2[:, l, :, :], psi_w2[l].rearrange("(h p) d -> p h d", p=P)))
            assert len(loads) == N_W
            for to, of in loads:
                sp.dma_start(to, of).then_inc(s_w, 16)
            sp.wait_ge(s_pool0, 1)
            sp.dma_start(bf2_row[0:3, :], b_f2.to_broadcast([3, D])).then_inc(s_w, 16)

            def store_tables(n, k):
                for half in range(2):
                    q = (n * CHUNKS + k) * 2 + half
                    r = k * CT + 2 * half
                    sp.wait_ge(s_bev, q + 1)
                    sp.dma_start(B_d[n][bass.ds(r * P, 2 * P), :].rearrange("(t p) f -> p t f", p=P),
                                 Bst[:, half, :, :]).then_inc(s_store[half], 16)
                    sp.wait_ge(s_am, q + 1)
                    sp.wait_ge(s_lo, q + 1)
                    sp.dma_start(A3_d[n][bass.ds(r * P * 3, 2 * P * 3), :].rearrange(
                                     "(t p c) f -> p t (c f)", p=P, c=3),
                                 A3st[:, half, :, :, :].rearrange("p t c f -> p t (c f)")
                                 ).then_inc(s_store[half], 16)

            def stored(eng, n):
                for half in range(2):
                    eng.wait_ge(s_store[half], (n + 1) * CHUNKS * 32)

            def load_window(l, g, u):
                c = l * GROUPS + g
                if not (isinstance(c, int) and c < UNROLL):
                    sp.wait_ge(s_X, c - UNROLL + 1)
                b = sp.value_load(base_i[0:1, bass.ds(g, 1)], min_val=0, max_val=NODES)
                table, width = (A3_d[l], H) if l < LAYERS else (hf3_d, D)
                sp.dma_start(A3[:, u, 0:width], table[bass.ds(b * 3, WIN3), :]).then_inc(s_win[u], 16)

            with nc.allow_non_contiguous_dma(reason="rows of a table"):
                with sp.Fori(0, CHUNKS, 1) as k:
                    store_tables(0, k)
                sp.wait_ge(s_c, 6)
                for l in range(LAYERS):
                    stored(sp, l)
                    for u in range(UNROLL):
                        load_window(l, u, u)
                    with sp.Fori(1, GROUPS // UNROLL, 1) as i:
                        for u in range(UNROLL):
                            load_window(l, i * UNROLL + u, u)
                    with sp.If(any_outside(sp)):
                        sp.wait_ge(s_acc, (l + 1) * GROUPS)
                        with sp.Fori(1, EDGE_TILES + 1, 1) as t:
                            sp.wait_ge(s_far_idx, l * EDGE_TILES + t)
                            sp.dma_start(far_i[:, 0:1], dst[:, bass.ds(t - 1, 1)]).then_inc(s_far_dst, 16)
                    if l < LAYERS - 1:
                        with sp.Fori(0, CHUNKS, 1) as k:
                            store_tables(l + 1, k)
                sp.wait_ge(s_acc, LAYERS * GROUPS)
                def load_x_rows(k):
                    sp.dma_start(xres.rearrange("p (t d) -> p t d", d=D),
                                 xN[chunk(k), :].rearrange("(t p) d -> p t d", p=P)).then_inc(s_xres, 16)

                load_x_rows(0)
                with sp.Fori(1, CHUNKS, 1) as k:
                    sp.wait_ge(s_y, k)
                    load_x_rows(k)
                sp.dma_start(rcut_t, rcut).then_inc(s_rcut, 16)
                with sp.Fori(0, CHUNKS, 1) as k:
                    sp.wait_ge(s_hlo, k + 1)
                    sp.dma_start(hf3_d[bass.ds(k * CHUNK * 3, CHUNK * 3), :].rearrange(
                                     "(t p c) f -> p t (c f)", p=P, c=3),
                                 H3st.rearrange("p t c f -> p t (c f)")).then_inc(s_xres, 16)
                def load_f(i, u):
                    g = i * UNROLL + u
                    if not (isinstance(g, int) and g < UNROLL):
                        sp.wait_ge(s_Z, g - UNROLL + 1)
                    sp.dma_start(fbuf[:, u, :], fT[:, bass.ds(g * GROUP, GROUP)]).then_inc(s_f[u], 16)

                sp.wait_ge(s_xres, 32 * CHUNKS)
                sp.wait_ge(s_place, 1)
                with sp.If(any_outside(sp)):
                    with sp.Fori(1, EDGE_TILES + 1, 1) as t:
                        sp.wait_ge(s_far_idx, LAYERS * EDGE_TILES + t)
                        sp.dma_start(far_i[:, 0:1], dst[:, bass.ds(t - 1, 1)]).then_inc(s_far_dst, 16)
                        sp.wait_ge(s_far_hf, t)
                        sp.dma_start(hf_edge_d[bass.ds((t - 1) * P, P), :], far_hf).then_inc(s_far_out, 16)
                for u in range(UNROLL):
                    load_f(0, u)
                    load_window(LAYERS, u, u)
                with sp.Fori(1, GROUPS // UNROLL, 1) as i:
                    for u in range(UNROLL):
                        load_f(i, u)
                        load_window(LAYERS, i * UNROLL + u, u)
                load_f(GROUPS // UNROLL, 0)

                def load_rows(i, u):
                    g = i * SLOTS + u
                    if not (isinstance(g, int) and g < SLOTS):
                        sp.wait_ge(s_seg1, g - SLOTS + 1)
                    sp.dma_start(sorted_rows[:, u, :, :], sorted_d[bass.ds(g * GROUP, GROUP), :].rearrange(
                        "(t p) w -> p t w", p=P)).then_inc(s_row[u], 16)

                for u in range(UNROLL):
                    sp.wait_ge(s_G[u], (LAYERS + 1) * (GROUPS // UNROLL) * TILES * 16)
                sp.wait_ge(s_clear, 16 * CLEARS)
                for u in range(SLOTS):
                    load_rows(0, u)
                with sp.Fori(1, SORTED // SLOTS, 1) as i:
                    for u in range(SLOTS):
                        load_rows(i, u)

                with sp.Fori(0, FULL_TILES // CT, 1) as k:
                    sp.wait_ge(s_norm, k + 1)
                    sp.dma_start(out[chunk(k), :].rearrange("(t p) d -> p t d", p=P),
                                 x1[:, bass.ds(k * CT, CT), :]).then_inc(s_out, 16)
                sp.wait_ge(s_norm, CHUNKS)
                sp.dma_start(out[FULL_TILES * P:NODES, :], x1[0:REST, FULL_TILES, :]).then_inc(s_out, 16)
                sp.wait_ge(s_out, 16 * CHUNKS)

        @block.gpsimd
        def _(pool):
            pool.memset(bf2_row[:, :], 0.0).then_inc(s_pool0, 1)
            pool.memset(first_row[:, :], 0.0).then_inc(s_pool0, 1)
            pool.memset(S[:, :, :], 0.0)
            pool.memset(ident[:, :], 0.0).then_inc(s_pool0, 1)
            pool.memset(ones[:, :], 1.0).then_inc(s_pool0, 1)
            pool.iota(iota1[:, :], pattern=[[1, WIN]], base=0, channel_multiplier=0,
                      allow_small_or_imprecise_dtypes=True).then_inc(s_pool0, 1)
            pool.iota(iota3[:, :], pattern=[[1, WIN], [0, 3]], base=0, channel_multiplier=0,
                      allow_small_or_imprecise_dtypes=True).then_inc(s_pool0, 1)
            pool.memset(zeros[:, :], 0.0).then_inc(s_pool0, 1)
            pool.iota(iota_b[:, :], pattern=[[1, NB]], base=0, channel_multiplier=0,
                      allow_small_or_imprecise_dtypes=True).then_inc(s_pool0, 1)
            pool.memset(below[:, :], 1.0).then_inc(s_pool0, 1)
            pool.memset(not_below[:, :], 1.0).then_inc(s_pool0, 1)
            pool.wait_ge(s_pool0, 10)
            pool.affine_select(out=below[:, :], in_=below[:, :], compare_op=ALU.is_ge, fill=0.0,
                               base=-1, pattern=[[1, P]], channel_multiplier=-1).then_inc(s_pool0, 1)
            pool.affine_select(out=not_below[:, :], in_=not_below[:, :], compare_op=ALU.is_ge, fill=0.0,
                               base=0, pattern=[[-1, P]], channel_multiplier=1).then_inc(s_pool0, 1)
            pool.affine_select(out=ident[:, :], in_=ident[:, :], compare_op=ALU.not_equal, fill=1.0,
                               base=0, pattern=[[-1, P]], channel_multiplier=1).then_inc(s_pool0, 1)
            pool.memset(first_row[0:1, :], 1.0).then_inc(s_pool0, 1)
            pool.memset(agg[:, :, :], 0.0).then_inc(s_zero, 1)

            last_row = pool.alloc_register("last_row")
            row_before = pool.alloc_register("row_before")
            pool.reg_mov(row_before, NPAD - 2)

            def third_part(n, k):
                for half in range(2):
                    q = (n * CHUNKS + k) * 2 + half
                    pool.wait_ge(s_am, q + 1)
                    pool.tensor_tensor(out=A3st[:, half, :, 2, :], in0=Ar, in1=A3st[:, half, :, 1, :],
                                       op=ALU.subtract).then_inc(s_lo, 1)

            def rows_in_out(l, i):
                for u in range(UNROLL):
                    c = l * GROUPS + i * UNROLL + u
                    if u % 2 == 0:
                        pool.wait_ge(s_idx, l * (GROUPS // 2) + i * 2 + u // 2 + (1 if l < LAYERS else 3))
                    if l < LAYERS and not (isinstance(c, int) and c < UNROLL):
                        pool.wait_ge(s_add, c - UNROLL + 1)
                    if l == LAYERS:
                        pool.wait_ge(s_prod, i * UNROLL + u + 1)
                    pool.reg_add(last_row, row_before, 1)
                    for j in range(TILES):
                        at = bass.IndirectOffsetOnAxis(ap=idx[:, u * TILES + j:u * TILES + j + 1], axis=0)
                        if l < LAYERS:
                            pool.indirect_dma_start(
                                out=G[:, u, j * H:(j + 1) * H], out_offset=None, in_=B_d[l][:, :], in_offset=at,
                                bounds_check=last_row, oob_is_err=False).then_inc(s_G[u], 16)
                        else:
                            pool.indirect_dma_start(
                                out=sorted_d[:, :], out_offset=at, in_=rows[:, u, j, :], in_offset=None,
                                bounds_check=last_row, oob_is_err=False).then_inc(s_G[u], 16)

            with pool.Fori(0, CHUNKS, 1) as k:
                third_part(0, k)
            for l in range(LAYERS):
                for half in range(2):
                    pool.wait_ge(s_store[half], (l + 1) * CHUNKS * 32)
                rows_in_out(l, 0)
                with pool.Fori(1, GROUPS // UNROLL, 1) as i:
                    rows_in_out(l, i)
                with pool.If(any_outside(pool)):
                    pool.wait_ge(s_acc, (l + 1) * GROUPS)
                    pool.iota(far_iota, pattern=[[1, CHUNK]], base=0, channel_multiplier=0,
                              allow_small_or_imprecise_dtypes=True).then_inc(s_far_iota, 1)
                    with pool.Fori(0, EDGE_TILES, 1) as t:
                        pool.wait_ge(s_far_idx, l * EDGE_TILES + t + 2)
                        pool.reg_add(last_row, row_before, 1)
                        pool.indirect_dma_start(
                            out=far_B, out_offset=None, in_=B_d[l][:, :],
                            in_offset=bass.IndirectOffsetOnAxis(ap=far_i[:, 2:3], axis=0),
                            bounds_check=last_row, oob_is_err=False).then_inc(s_far_rows[l], 16)
                        pool.indirect_dma_start(
                            out=far_A3.rearrange("p c f -> p (c f)"), out_offset=None,
                            in_=A3_d[l].rearrange("(n c) f -> n (c f)", c=3),
                            in_offset=bass.IndirectOffsetOnAxis(ap=far_i[:, 1:2], axis=0),
                            bounds_check=last_row, oob_is_err=False).then_inc(s_far_rows[l], 16)
                if l < LAYERS - 1:
                    with pool.Fori(0, CHUNKS, 1) as k:
                        pool.wait_ge(s_z, l * CHUNKS + k + 1)
                        pool.tensor_copy(agg[:, 0, chunk(k)], zeros[:, 0:1].to_broadcast([P, CHUNK])).then_inc(s_zero, 1)
                        pool.tensor_copy(agg[:, 1, chunk(k)], zeros[:, 0:1].to_broadcast([P, CHUNK])).then_inc(s_zero, 1)
                        third_part(l + 1, k)
            with pool.Fori(0, CHUNKS, 1) as k:
                pool.wait_ge(s_z, (LAYERS - 1) * CHUNKS + k + 1)
                pool.tensor_copy(agg[:, 0, chunk(k)], zeros[:, 0:1].to_broadcast([P, CHUNK])).then_inc(s_zero, 1)
            pool.iota(iota_t, pattern=[[1, SORTED]], base=0, channel_multiplier=0,
                      allow_small_or_imprecise_dtypes=True).then_inc(s_zero, 1)
            pool.memset(zero_rows, 0.0).then_inc(s_zero, 1)

            def mask_prefixes(k, first=False):
                for n in range(PER_CHUNK):
                    at = k * PER_CHUNK + n
                    pool.wait_ge(s_ps, at + 1)
                    if not (first and n < 2):
                        pool.wait_ge(s_pick, at - 1)
                    pool.tensor_tensor(out=picked[:, n % 2, :, :], in0=one_bucket[:, n % 4, :, :],
                                       in1=prefix[:, n % 2, :].unsqueeze(1).to_broadcast([P, STEP, NB]),
                                       op=ALU.mult).then_inc(s_mul, 1)
                pool.wait_ge(s_hs, 3 * k + 3)
                pool.tensor_tensor(out=H3st[:, :, 2, :], in0=xres_t, in1=H3st[:, :, 1, :],
                                   op=ALU.subtract).then_inc(s_hlo, 1)

            mask_prefixes(0, first=True)
            with pool.Fori(1, CHUNKS, 1) as k:
                mask_prefixes(k)
            pool.wait_ge(s_clear, 16 * CLEARS)
            with pool.If(any_outside(pool)):
                pool.wait_ge(s_xres, 32 * CHUNKS)
                with pool.Fori(0, EDGE_TILES, 1) as t:
                    pool.wait_ge(s_far_idx, LAYERS * EDGE_TILES + t + 2)
                    pool.reg_add(last_row, row_before, 1)
                    pool.indirect_dma_start(
                        out=far_hf3.rearrange("p c f -> p (c f)"), out_offset=None,
                        in_=hf3_d.rearrange("(n c) f -> n (c f)", c=3),
                        in_offset=bass.IndirectOffsetOnAxis(ap=far_i[:, 1:2], axis=0),
                        bounds_check=last_row, oob_is_err=False).then_inc(s_far_rows[LAYERS], 16)
            pool.reg_mov(row_before, (SPARE + NB) * GROUP - 2)
            rows_in_out(LAYERS, 0)
            with pool.Fori(1, GROUPS // UNROLL, 1) as i:
                rows_in_out(LAYERS, i)

        @block.scalar
        def _(act):
            act.preload_act_table_set("natural_log_exp_and_others")
            act.wait_ge(s_w, 16 * (N_W + 1))
            act.wait_ge(s_c, 6)

            def copy_B(n, k):
                for half in range(2):
                    q = (n * CHUNKS + k) * 2 + half
                    act.wait_ge(s_at, 3 * q + 1)
                    if not (isinstance(q, int) and q < 2):
                        act.wait_ge(s_store[half], (n * CHUNKS + k) * 32)
                    act.activation(Bst[:, half, :, :], tab_bank[half][:, :, H:2 * H], ACT.Copy).then_inc(s_bev, 1)

            def hotT_copy(c, s):
                act.wait_ge(s_tr, c + 1)
                if not (isinstance(c, int) and c < 2):
                    act.wait_ge(s_X, c - 1)
                act.activation(hotT[:, s, :], PTb[s][0:WIN3, 0:GROUP], ACT.Copy).then_inc(s_hotT, 1)

            def copy_sums(l, c, s):
                n = 3 if l == 0 else 2
                act.wait_ge(s_seg, c + 1)
                if not (isinstance(c, int) and c < 1):
                    act.wait_ge(s_back, c)
                act.activation(S[0:WIN, 0:n, :], PO[0:WIN, s, 0:n * P].rearrange("w (h f) -> w h f", h=n),
                               ACT.Copy).then_inc(s_S, 1)

            def edge_step(l, g, u, behind=True):
                c = l * GROUPS + g
                if behind:
                    copy_sums(l, c - 2, u % 2)
                hotT_copy(c + 1, (u + 1) % 2)
                act.wait_ge(s_add, c + 1)
                act.activation(M[:, u % 2, :], M[:, u % 2, :], ACT.Relu).then_inc(s_M, 1)

            def node_step(l, k, first=False):
                kk = l * CHUNKS + k
                act.wait_ge(s_u, kk + 1)
                act.activation(u_b[:, 0, :], PX[:, 1, :], ACT.Relu, bias=c1_col[:, l, 0:1]).then_inc(s_ur, 1)
                act.activation(u_b[:, 1, :], PX[:, 2, :], ACT.Relu, bias=c1_col[:, l, 1:2]).then_inc(s_ur, 1)
                if l == 0:
                    act.wait_ge(s_pr, k + 1)
                    if not first:
                        act.wait_ge(s_h, k)
                    act.activation(xres, PX[:, 1, :], ACT.Copy).then_inc(s_prc, 1)
                if l < LAYERS - 1 and not first:
                    if l == 0:
                        keep(k - 1)
                    copy_B(l + 1, k - 1)

            def keep(k):
                act.wait_ge(s_h, k + 1)
                act.activation(hT[:, chunk(k)], h_b, ACT.Copy).then_inc(s_keep, 1)

            act.wait_ge(s_tab, 48)
            act.activation(h_b, hT[:, 0:CHUNK], ACT.Copy).then_inc(s_x0, 1)
            act.wait_ge(s_tp, 2)
            act.activation(h_b, hT[:, CHUNK:2 * CHUNK], ACT.Copy).then_inc(s_x0, 1)
            copy_B(0, 0)
            with act.Fori(1, CHUNKS - 1, 1) as k:
                act.wait_ge(s_tp, 2 * k + 2)
                act.activation(h_b, hT[:, bass.ds((k + 1) * CHUNK, CHUNK)], ACT.Copy).then_inc(s_x0, 1)
                copy_B(0, k)
            copy_B(0, CHUNKS - 1)
            hotT_copy(0, 0)
            for l in range(LAYERS):
                for u in range(UNROLL):
                    edge_step(l, u, u, behind=u >= 2)
                with act.Fori(1, GROUPS // UNROLL, 1) as i:
                    for u in range(UNROLL):
                        edge_step(l, i * UNROLL + u, u)
                for n in (2, 1):
                    copy_sums(l, (l + 1) * GROUPS - n, n % 2)
                node_step(l, 0, first=True)
                with act.Fori(1, CHUNKS, 1) as k:
                    node_step(l, k)
                if l == 0:
                    keep(CHUNKS - 1)
                if l < LAYERS - 1:
                    copy_B(l + 1, CHUNKS - 1)
            act.wait_ge(s_var, 1)
            act.activation(std[:, :], veps[:, :], ACT.Sqrt).then_inc(s_std, 1)
            act.preload_act_table_set("natural_log_exp_and_others")
            act.wait_ge(s_list, 1)
            act.wait_ge(s_zero, 3 + (2 * LAYERS - 1) * CHUNKS)

            def copies_of_chunk(k, first=False):
                act.wait_ge(s_x1p, k + 1)
                act.activation(m_b, PX[:, 0, :], ACT.Copy).then_inc(s_x1T, 1)
                for n in range(PER_CHUNK):
                    at = k * PER_CHUNK + n
                    act.wait_ge(s_pre, at + 1)
                    if not (first and n < 2):
                        act.wait_ge(s_mul, at - 1)
                    act.activation(prefix[:, n % 2, :], PX[:, 3, 0:NB], ACT.Copy).then_inc(s_ps, 1)
                    to = act.value_load(zero_list[0:1, bass.ds(at, 1)], min_val=0, max_val=SPARE + NB - 1)
                    act.dma_start(sorted_d[bass.ds(to * GROUP, GROUP), :].rearrange("(t p) w -> p t w", p=P),
                                  zero_rows.unsqueeze(1).to_broadcast([P, TILES, ROW])).then_inc(s_clear, 16)

            copies_of_chunk(0, first=True)
            with act.Fori(1, CHUNKS, 1) as k:
                copies_of_chunk(k)

            def softplus_parts(c, s):
                act.wait_ge(s_Z, c + 1)
                act.activation(a_b, PX[:, s, :], ACT.Abs, bias=bf1_col[:, 0:1]).then_inc(s_abs, 1)
                act.wait_ge(s_abs, c + 1)
                act.activation(e_b, a_b, ACT.Exp, scale=-1.0).then_inc(s_exp, 1)
                act.wait_ge(s_exp, c + 1)
                if not (isinstance(c, int) and c < 1):
                    act.wait_ge(s_sp, c)
                act.activation(l_b, e_b, ACT.Ln, bias=1.0).then_inc(s_ln, 1)

            def filter_step(i, u, far=False):
                g = i * UNROLL + u
                hotT_copy(LAYERS * GROUPS + g + 1, (u + 1) % 2)
                act.wait_ge(s_X, LAYERS * GROUPS + g + 1)
                if not (isinstance(g, int) and g < 2):
                    act.wait_ge(s_prod, g - 1)
                if far:
                    if not (isinstance(g, int) and g < 1):
                        act.wait_ge(s_xj, g)
                    act.dma_start(xj_far.rearrange("p (t d) -> p t d", d=D),
                                  hf_edge_d[bass.ds(g * GROUP, GROUP), :].rearrange(
                                      "(t p) d -> p t d", p=P)).then_inc(s_far_xj, 16)
                    act.wait_ge(s_far_xj, (g + 1) * 16)
                    act.activation(xj_b[:, u % 2, :], xj_far, ACT.Copy).then_inc(s_xj, 1)
                else:
                    act.activation(xj_b[:, u % 2, :], PO[:, u % 2, :], ACT.Copy).then_inc(s_xj, 1)
                softplus_parts(g + 1, (u + 1) % 2)

            act.wait_ge(s_place, 1)
            softplus_parts(0, 0)
            with act.If(any_outside(act)):
                act.wait_ge(s_far_out, 16 * EDGE_TILES)
                for u in range(UNROLL):
                    filter_step(0, u, far=True)
                with act.Fori(1, GROUPS // UNROLL, 1) as i:
                    for u in range(UNROLL):
                        filter_step(i, u, far=True)
            with act.Else():
                for u in range(UNROLL):
                    filter_step(0, u)
                with act.Fori(1, GROUPS // UNROLL, 1) as i:
                    for u in range(UNROLL):
                        filter_step(i, u)

            def out_softplus_parts(k, first=False):
                act.wait_ge(s_o1, k + 1)
                act.activation(m_b, PX[:, 0, :], ACT.Abs, bias=bo1_col[:, 0:1]).then_inc(s_oa, 1)
                act.wait_ge(s_oa, 3 * k + 1)
                act.activation(t_b, m_b, ACT.Exp, scale=-1.0).then_inc(s_oa, 1)
                act.wait_ge(s_oa, 3 * k + 2)
                if not first:
                    act.wait_ge(s_osp, k)
                act.activation(xres, t_b, ACT.Ln, bias=1.0).then_inc(s_oa, 1)

            out_softplus_parts(0, first=True)
            with act.Fori(1, CHUNKS, 1) as k:
                out_softplus_parts(k)
            act.wait_ge(s_var, 2)
            act.activation(std[:, :], veps[:, :], ACT.Sqrt).then_inc(s_std, 1)

        @block.tensor
        def _(pe):
            pe.wait_ge(s_w, 16 * (N_W + 1))
            pe.wait_ge(s_pool0, 14)
            pe.wait_ge(s_c, 3)
            last = pe.matmul(PX[:, 0, 0:GROUPS + AHEAD], first_row[:, :], dst_f[:, 0:TABLE:TILES],
                             start=True, stop=True).then_inc(s_bb, 1)

            pe.wait_ge(s_os, 5)
            pe.matmul(PX[:, 1, 0:1], ones[:, :], outside[:, :], start=True, stop=True).then_inc(s_osum, 1)

            def tables(n, k):
                if n == 0:
                    pe.wait_ge(s_x0, k + 1)
                else:
                    pe.wait_ge(s_h, (n - 1) * CHUNKS + k + 1)
                for half in range(2):
                    q = (n * CHUNKS + k) * 2 + half
                    if not (isinstance(q, int) and q < 2):
                        pe.wait_ge(s_bev, q - 1)
                        pe.wait_ge(s_am, q - 1)
                    for t in range(2):
                        mm = pe.matmul(tab_bank[half][:, t, :],
                                       h_b[:, (2 * half + t) * P:(2 * half + t + 1) * P],
                                       w1[:, n, :], start=True, stop=True)
                    mm.then_inc(s_tp, 1)

            def transposes(c, s):
                pe.wait_ge(s_hot, c + 1)
                if not (isinstance(c, int) and c < 2):
                    pe.wait_ge(s_hotT, c - 1)
                for j in range(TILES):
                    mm = pe.transpose(PTb[s][0:WIN3, j * P:(j + 1) * P], hot3[:, s, j, :], ident_b[:, :])
                mm.then_inc(s_tr, 1)

            def sum_messages(l, c, s, u4):
                pe.wait_ge(s_M, c + 1)
                if not (isinstance(c, int) and c < 2):
                    pe.wait_ge(s_acc, c - 1)
                for j in range(TILES):
                    mm = pe.matmul(PO[0:WIN, s, 0:H], hot[:, u4, j, :], M[:, s, j * H:(j + 1) * H],
                                   start=(j == 0), stop=(j == TILES - 1))
                if l == 0:
                    for j in range(TILES):
                        mm = pe.matmul(PO[0:WIN, s, H:H + P], hot[:, u4, j, :].bitcast(BF16)[:, 1::2],
                                       ones_b[:, :], start=(j == 0), stop=(j == TILES - 1))
                mm.then_inc(s_seg, 1)

            def sums_back(l, c, s):
                pe.wait_ge(s_S, c + 1)
                for h in range(3 if l == 0 else 2):
                    mm = pe.matmul(PO[:, s, 3 * P + h * WIN:3 * P + (h + 1) * WIN], S[:, h, :],
                                   ident[:, 0:WIN], start=True, stop=True)
                mm.then_inc(s_back, 1)

            def edge_step(l, i, u, first=False, behind=True):
                c = l * GROUPS + i * UNROLL + u
                pe.wait_ge(s_hotT, c + 1)
                pe.wait_ge(s_win[u], (l * (GROUPS // UNROLL) + i + 1) * 16)
                if not (isinstance(c, int) and c < 2):
                    pe.wait_ge(s_add, c - 1)
                for j in range(TILES):
                    mm = pe.matmul(PX[:, 2 * (u % 2) + j // 2, (j % 2) * H:(j % 2 + 1) * H],
                                   hotT[:, u % 2, j * P:(j + 1) * P], A3[:, u, :], start=True, stop=True)
                mm.then_inc(s_X, 1)
                transposes(c + 1, (u + 1) % 2)
                if behind:
                    sums_back(l, c - 2, u % 2)
                if not first:
                    sum_messages(l, c - 1, (u - 1) % 2, (u - 1) % UNROLL)

            def edge_sums(l, k):
                for h in range(2):
                    mm = pe.matmul(PX[:, 0, :], w2[:, l, h, :], agg[:, h, chunk(k)], start=h == 0, stop=h == 1)
                mm.then_inc(s_z, 1)

            def node_step(l, k, first=False, last=False):
                kk = l * CHUNKS + k
                pe.wait_ge(s_m, kk + 1)
                if l == 0 and not first:
                    pe.wait_ge(s_prc, k)
                for h in range(2):
                    mm = pe.matmul(PX[:, 1 + h, :], v1[:, l, h * P:(h + 1) * P], m_b, start=True, stop=True)
                mm.then_inc(s_u, 1)
                if not last:
                    edge_sums(l, k + 1)
                pe.wait_ge(s_ur, 2 * kk + 2)
                if l == 0:
                    pe.matmul(PX[:, 1, :], pw[:, :], hT[:, chunk(k)], start=True, stop=True).then_inc(s_pr, 1)
                if l < LAYERS - 1 and not first:
                    tables(l + 1, k - 1)
                if l < LAYERS - 1:
                    for h in range(2):
                        mm = pe.matmul(PX[:, 3, :], v2[:, l, h, :], u_b[:, h, :], start=h == 0, stop=h == 1)
                else:
                    if not first:
                        pe.wait_ge(s_y, k)
                    for t in range(CT):
                        for h in range(2):
                            mm = pe.matmul(PX[:, 3, t * D:(t + 1) * D], u_b[:, h, t * P:(t + 1) * P],
                                           v2[:, l, h, :], start=h == 0, stop=h == 1)
                mm.then_inc(s_v, 1)

            pe.wait_ge(s_c, 6)
            pe.wait_ge(s_os, 6)
            tables(0, 0)
            with pe.Fori(1, CHUNKS, 1) as k:
                tables(0, k)
            pe.wait_ge(s_bev, 2 * CHUNKS)
            pe.wait_ge(s_am, 2 * CHUNKS)
            transposes(0, 0)
            for l in range(LAYERS):
                for u in range(UNROLL):
                    edge_step(l, 0, u, first=u == 0, behind=u >= 2)
                with pe.Fori(1, GROUPS // UNROLL, 1) as i:
                    for u in range(UNROLL):
                        edge_step(l, i, u)
                sums_back(l, (l + 1) * GROUPS - 2, 0)
                sum_messages(l, (l + 1) * GROUPS - 1, 1, UNROLL - 1)
                sums_back(l, (l + 1) * GROUPS - 1, 1)
                pe.wait_ge(s_acc, (l + 1) * GROUPS)
                pe.wait_ge(s_hotT, (l + 1) * GROUPS + 1)
                with pe.If(any_outside(pe)):
                    sums = 3 if l == 0 else 2
                    with pe.Fori(0, EDGE_TILES, 1) as t:
                        with pe.Fori(0, CHUNKS, 1) as k:
                            n = (l * EDGE_TILES + t) * CHUNKS + k
                            pe.wait_ge(s_far_hot, n + 1)
                            for h in range(2):
                                mm = pe.matmul(PX[:, h, :], far_m[:, h * P:(h + 1) * P], far_hot,
                                               start=True, stop=True)
                            if l == 0:
                                mm = pe.matmul(PX[:, 2, :], ones[:, :], far_hot, start=True, stop=True)
                            mm.then_inc(s_far_seg, 1)
                    pe.wait_ge(s_far_acc, (l + 1) * EDGE_TILES * CHUNKS)
                edge_sums(l, 0)
                node_step(l, 0, first=True)
                with pe.Fori(1, CHUNKS - 1, 1) as k:
                    node_step(l, k)
                node_step(l, CHUNKS - 1, last=True)
                if l < LAYERS - 1:
                    tables(l + 1, CHUNKS - 1)
                else:
                    pe.wait_ge(s_y, CHUNKS)
                if l < LAYERS - 1:
                    pe.wait_ge(s_bev, 2 * CHUNKS * (l + 2))
                    pe.wait_ge(s_am, 2 * CHUNKS * (l + 2))
            def hidden(g, s, u4, step):
                pe.wait_ge(s_f[u4], (step + 1) * 16)
                if not (isinstance(g, int) and g < 2):
                    pe.wait_ge(s_abs, g - 1)
                    pe.wait_ge(s_q, g - 1)
                pe.matmul(PX[:, s, :], wf1[:, :], fbuf[:, u4, :], start=True, stop=True).then_inc(s_Z, 1)

            pe.wait_ge(s_cnt, NB)
            pe.matmul(PX[:, 0, 0:NB], ones[:, :], many, start=True, stop=True).then_inc(s_tot, 1)
            pe.wait_ge(s_start, 1)
            pe.matmul(PX[:, 3, 0:NB], first_row[:, :], starts, start=True, stop=True, skip_group_check=True)
            pe.matmul(PX[0:NB, 2, 0:1], ends_last, first_row[:, 0:1], start=True, stop=True).then_inc(s_run, 1)
            pe.wait_ge(s_mask, 1)
            pe.matmul(PX[:, 2, 0:SORTED], ones[0:NB, :], M[0:NB, 0, 0:SORTED], start=True, stop=True).then_inc(s_tb, 1)

            def sort_step(n, s):
                pe.wait_ge(s_ob, n + 1)
                for t in range(STEP):
                    mm = pe.matmul(PX[:, 3, 0:NB], below[:, :], one_bucket[:, s, t, :],
                                   start=False, stop=True, skip_group_check=True)
                mm.then_inc(s_pre, 1)
                pe.wait_ge(s_ps, n + 1)
                for t in range(STEP):
                    mm = pe.matmul(PX[:, 3, 0:NB], not_below[:, :], one_bucket[:, s, t, :],
                                   start=False, stop=True, skip_group_check=True)
                mm.then_inc(s_cum, 1)

            with pe.Fori(0, CHUNKS, 1) as k:
                pe.wait_ge(s_x1, k + 1)
                for t in range(CT):
                    mm = pe.transpose(PX[:, 0, t * P:(t + 1) * P], x_b[:, t * D:(t + 1) * D], ident[:, :])
                mm.then_inc(s_x1p, 1)
                for n in range(PER_CHUNK):
                    if n == 2:
                        pe.wait_ge(s_x1T, k + 1)
                        for t in range(CT):
                            mm = pe.matmul(PX[:, 1, t * D:(t + 1) * D], m_b[:, t * P:(t + 1) * P], win2f[:, :],
                                           start=True, stop=True)
                        mm.then_inc(s_hf, 1)
                    sort_step(k * PER_CHUNK + n, n % 4)

            def filter_step(i, u):
                g = i * UNROLL + u
                c = LAYERS * GROUPS + g
                if u == UNROLL - 1:
                    hidden(g + 1, 0, 0, i + 1)
                else:
                    hidden(g + 1, (u + 1) % 2, u + 1, i)
                pe.wait_ge(s_hotT, c + 1)
                pe.wait_ge(s_win[u], (LAYERS * (GROUPS // UNROLL) + i + 1) * 16)
                if not (isinstance(g, int) and g < 2):
                    pe.wait_ge(s_xj, g - 1)
                    pe.wait_ge(s_prod, g - 1)
                for j in range(TILES):
                    mm = pe.matmul(PO[:, u % 2, j * D:(j + 1) * D], hotT[:, u % 2, j * P:(j + 1) * P],
                                   A3[:, u, 0:D], start=True, stop=True)
                mm.then_inc(s_X, 1)
                transposes(c + 1, (u + 1) % 2)
                pe.wait_ge(s_sp, g + 1)
                pe.matmul(PX[:, 2 + u % 2, :].rearrange("p (t d) -> p t d", d=D), ones_b[:, :],
                          bf2_3[:, :].unsqueeze(1).to_broadcast([P, TILES, D]),
                          start=True, stop=True, skip_group_check=True)
                for j in range(TILES):
                    mm = pe.matmul(PX[:, 2 + u % 2, j * D:(j + 1) * D], sp_b[:, u % 2, j * P:(j + 1) * P],
                                   wf2[:, :], start=False, stop=True, skip_group_check=True)
                mm.then_inc(s_Y, 1)

            hidden(0, 0, 0, 0)
            for u in range(UNROLL):
                filter_step(0, u)
            with pe.Fori(1, GROUPS // UNROLL, 1) as i:
                for u in range(UNROLL):
                    filter_step(i, u)
            pe.wait_ge(s_prod, GROUPS)
            pe.wait_ge(s_abs, GROUPS + 1)
            pe.wait_ge(s_q, GROUPS + 1)

            def sum_sorted(i, u):
                g = i * SLOTS + u
                pe.wait_ge(s_hot128, g + 1)
                if not (isinstance(g, int) and g < 3):
                    pe.wait_ge(s_acc1, g - 2)
                for j in range(TILES):
                    mm = pe.matmul(PX[:, u % 3, 0:P], sorted_rows[:, u, j, 0:D], hot128[:, u % 2, j, :],
                                   start=(j == 0), stop=(j == TILES - 1))
                mm.then_inc(s_seg1, 1)

            for u in range(SLOTS):
                sum_sorted(0, u)
            with pe.Fori(1, SORTED // SLOTS, 1) as i:
                for u in range(SLOTS):
                    sum_sorted(i, u)
            pe.wait_ge(s_acc1, SORTED)

            def out_hidden(k):
                pe.matmul(PX[:, 0, :], wo1[:, :], agg[:, 0, chunk(k)], start=True, stop=True).then_inc(s_o1, 1)

            def out_product(k, first=False):
                pe.wait_ge(s_osp, k + 1)
                if not first:
                    pe.wait_ge(s_oy, k)
                for t in range(CT):
                    mm = pe.matmul(PX[:, 3, t * D:(t + 1) * D], sp_b[:, 0, t * P:(t + 1) * P], wo2[:, :],
                                   start=True, stop=True)
                mm.then_inc(s_o2, 1)

            out_hidden(0)
            pe.wait_ge(s_oa, 1)
            pe.wait_ge(s_ot, 1)
            out_hidden(1)
            out_product(0, first=True)
            with pe.Fori(1, CHUNKS - 1, 1) as k:
                pe.wait_ge(s_oa, 3 * k + 1)
                pe.wait_ge(s_ot, k + 1)
                out_hidden(k + 1)
                out_product(k)
            out_product(CHUNKS - 1)

        @block.vector
        def _(dve):
            dve.wait_ge(s_w, 16 * (N_W + 1))
            dve.wait_ge(s_tab, 48)
            dve.wait_ge(s_pool0, 14)
            dve.tensor_copy(dst_f[:, :], G[:, 0, 0:TABLE].bitcast(I32)).then_inc(s_c, 1)
            dve.tensor_tensor(out=w1[:, :, 0:H], in0=w1[:, :, 0:H], in1=w1[:, :, H:2 * H],
                              op=ALU.subtract).then_inc(s_c, 1)
            bf2_steps = [0]

            def after_bf2(ins):
                bf2_steps[0] += 1
                ins.then_inc(s_bf2, 1)
                dve.wait_ge(s_bf2, bf2_steps[0])

            dve.tensor_copy(ones_b[:, :], ones[:, :])
            dve.tensor_copy(ident_b[:, :], ident[:, :]).then_inc(s_c, 1)
            dve.tensor_copy(idx[:, :], src_t[:, 0:UNROLL * TILES]).then_inc(s_idx, 2)
            parts, left = (M[:, 0, 0:2 * D].bitcast(BF16).rearrange("p (c d) -> p c d", c=4)[:, c, :]
                           for c in range(2)), M[:, 1, 0:D]
            high, mid = parts
            chosen = M[:, 1, D:2 * D]
            after_bf2(dve.tensor_copy(high, bf2_row[:, :]))
            after_bf2(dve.tensor_tensor(out=left, in0=bf2_row[:, :], in1=high, op=ALU.subtract))
            after_bf2(dve.tensor_copy(mid, left))
            after_bf2(dve.tensor_tensor(out=left, in0=left, in1=mid, op=ALU.subtract))
            after_bf2(dve.tensor_scalar(chosen, high, ident[:, 0:1], None, ALU.mult))
            after_bf2(dve.scalar_tensor_tensor(out=chosen, in0=mid, scalar=ident[:, 1:2], in1=chosen,
                                               op0=ALU.mult, op1=ALU.add))
            after_bf2(dve.scalar_tensor_tensor(out=bf2_3[:, :], in0=left, scalar=ident[:, 2:3], in1=chosen,
                                               op0=ALU.mult, op1=ALU.add))
            dve.wait_ge(s_bb, 1)
            bases = PX[:, 0, 0:GROUPS + AHEAD]
            dve.tensor_copy(base_i[:, :], bases[0:1, :]).then_inc(s_c, 1)
            dve.tensor_copy(G[:, 1, 0:GROUPS + AHEAD], bases).then_inc(s_c, 1)
            dve.wait_ge(s_c, 5)
            by_tile = dst_f[:, :].rearrange("p (g j) -> p g j", j=TILES)
            real, below0, out_f = M[:, 0, 0:TABLE], M[:, 1, 0:TABLE], G[:, 2, 0:TABLE]
            dve.tensor_scalar(real, dst_f[:, :], 0.0, None, ALU.is_ge).then_inc(s_os, 1)
            dve.wait_ge(s_os, 1)
            dve.tensor_tensor(out=by_tile, in0=by_tile,
                              in1=G[:, 1, 0:GROUPS + AHEAD].unsqueeze(2).to_broadcast([P, GROUPS + AHEAD, TILES]),
                              op=ALU.subtract).then_inc(s_c, 1)
            dve.wait_ge(s_c, 6)
            dve.tensor_scalar(below0, dst_f[:, :], 0.0, None, ALU.is_lt).then_inc(s_os, 1)
            dve.wait_ge(s_os, 2)
            dve.scalar_tensor_tensor(out=out_f, in0=dst_f[:, :], scalar=float(WIN), in1=below0,
                                     op0=ALU.is_ge, op1=ALU.add).then_inc(s_os, 1)
            dve.wait_ge(s_os, 3)
            dve.tensor_tensor(out=out_f, in0=out_f, in1=real, op=ALU.mult).then_inc(s_os, 1)
            dve.wait_ge(s_os, 4)
            dve.tensor_scalar(real, out_f, 1.0, 0.0, ALU.mult, ALU.add, accum_out=outside[:, :]).then_inc(s_os, 1)
            dve.wait_ge(s_osum, 1)
            dve.tensor_copy(outside_i[:, :], PX[:, 1, 0:1]).then_inc(s_os, 1)
            dve.tensor_copy(far_f[:, 0:1], outside[:, :]).then_inc(s_far_idx, 1)

            def far_indices(n, t, by_source=True):
                dve.wait_ge(s_far_dst, 16 * (n + 1))
                if by_source:
                    dve.tensor_copy(far_i[:, 2:3], src_t[:, bass.ds(t, 1)])
                dve.tensor_scalar(far_i[:, 1:2], far_i[:, 0:1], 0, None, ALU.max)

            def far_edges(l):
                with dve.If(any_outside(dve)):
                    dve.wait_ge(s_acc, (l + 1) * GROUPS)
                    dve.wait_ge(s_far_iota, l + 1)
                    with dve.Fori(0, EDGE_TILES, 1) as t:
                        n = l * EDGE_TILES + t
                        step = 5 * n
                        far_indices(n, t)
                        dve.tensor_copy(far_f[:, 0:1], far_i[:, 0:1])
                        dve.tensor_scalar(far_f[:, 1:2], dst_f[:, bass.ds(t, 1)], 0.0, None,
                                          ALU.is_lt).then_inc(s_far_step, 1)
                        dve.wait_ge(s_far_step, step + 1)
                        dve.scalar_tensor_tensor(out=far_f[:, 2:3], in0=dst_f[:, bass.ds(t, 1)],
                                                 scalar=float(WIN), in1=far_f[:, 1:2],
                                                 op0=ALU.is_ge, op1=ALU.add).then_inc(s_far_step, 1)
                        dve.wait_ge(s_far_step, step + 2)
                        dve.scalar_tensor_tensor(out=far_f[:, 3:4], in0=far_f[:, 0:1], scalar=1.0,
                                                 in1=far_f[:, 2:3], op0=ALU.add,
                                                 op1=ALU.mult).then_inc(s_far_idx, 1)
                        dve.wait_ge(s_far_idx, n + 2)
                        dve.tensor_scalar(far_f[:, 3:4], far_f[:, 3:4], -1.0, None, ALU.add)
                        dve.wait_ge(s_far_rows[l], 32 * (t + 1))
                        dve.tensor_tensor(out=far_m, in0=far_A3[:, 0, :], in1=far_A3[:, 1, :],
                                          op=ALU.add).then_inc(s_far_step, 1)
                        dve.wait_ge(s_far_step, step + 3)
                        dve.tensor_tensor(out=far_m, in0=far_m, in1=far_A3[:, 2, :],
                                          op=ALU.add).then_inc(s_far_step, 1)
                        dve.wait_ge(s_far_step, step + 4)
                        dve.tensor_tensor(out=far_m, in0=far_m, in1=far_B, op=ALU.add).then_inc(s_far_step, 1)
                        dve.wait_ge(s_far_step, step + 5)
                        dve.tensor_scalar(far_m, far_m, 0.0, None, ALU.max)
                        with dve.Fori(0, CHUNKS, 1) as k:
                            m = n * CHUNKS + k
                            dve.tensor_scalar(far_hot, far_iota, far_f[:, 3:4], None,
                                              ALU.is_equal).then_inc(s_far_hot, 1)
                            dve.wait_ge(s_far_hot, m + 1)
                            dve.tensor_scalar(far_f[:, 3:4], far_f[:, 3:4], -float(CHUNK), None, ALU.add)
                            dve.wait_ge(s_far_seg, m + 1)
                            for h in range(3 if l == 0 else 2):
                                part_sum = agg[:, h, bass.ds(k * CHUNK, CHUNK)]
                                last = dve.tensor_tensor(out=part_sum, in0=part_sum, in1=PX[:, h, :], op=ALU.add)
                            last.then_inc(s_far_acc, 1)
                            dve.wait_ge(s_far_acc, m + 1)

            def far_filter_rows():
                def tile(t):
                    far_indices(LAYERS * EDGE_TILES + t, t, by_source=False)
                    dve.tensor_copy(far_f[:, 0:1], far_i[:, 0:1]).then_inc(s_far_idx, 1)
                    dve.wait_ge(s_far_rows[LAYERS], 16 * (t + 1))
                    if not (isinstance(t, int) and t < 1):
                        dve.wait_ge(s_far_out, 16 * t)
                    dve.tensor_tensor(out=far_hf, in0=far_hf3[:, 0, :], in1=far_hf3[:, 1, :],
                                      op=ALU.add).then_inc(s_far_step, 1)
                    dve.wait_ge(s_far_step, 5 * LAYERS * EDGE_TILES + t + 1)
                    dve.tensor_tensor(out=far_hf, in0=far_hf, in1=far_hf3[:, 2, :],
                                      op=ALU.add).then_inc(s_far_hf, 1)
                    dve.wait_ge(s_far_hf, t + 1)

                with dve.If(any_outside(dve)):
                    tile(0)
                    with dve.Fori(1, EDGE_TILES, 1) as t:
                        tile(t)

            def split_A(n, k):
                for half in range(2):
                    tt = n * CHUNKS + k
                    q = tt * 2 + half
                    dve.wait_ge(s_tp, q + 1)
                    dve.tensor_tensor(out=Af, in0=tab_bank[half][:, :, 0:H],
                                      in1=b1_bc[:, n:n + 1, :].to_broadcast([P, 2, H]), op=ALU.add).then_inc(s_at, 1)
                    if not (isinstance(q, int) and q < 2):
                        dve.wait_ge(s_store[half], tt * 32)
                    dve.wait_ge(s_at, q * 3 + 1)
                    dve.tensor_copy(A3st[:, half, :, 0, :], Af).then_inc(s_at, 1)
                    dve.wait_ge(s_at, q * 3 + 2)
                    if not (isinstance(q, int) and q < 1):
                        dve.wait_ge(s_lo, q)
                    dve.tensor_tensor(out=Ar, in0=Af, in1=A3st[:, half, :, 0, :], op=ALU.subtract).then_inc(s_at, 1)
                    dve.wait_ge(s_at, q * 3 + 3)
                    dve.tensor_copy(A3st[:, half, :, 1, :], Ar).then_inc(s_am, 1)

            def build_hot(c, g, s, u4, sums=True):
                if not (isinstance(c, int) and c < 2):
                    dve.wait_ge(s_tr, c - 1)
                if sums and not (isinstance(c, int) and c < UNROLL):
                    dve.wait_ge(s_seg, c - UNROLL + 1)
                for j in range(TILES):
                    col = dst_f[:, bass.ds(g * TILES + j, 1)]
                    if sums:
                        dve.tensor_scalar(hot[:, u4, j, :], iota1[:, :], col, None, ALU.is_equal)
                    last = dve.tensor_scalar(hot3[:, s, j, :], iota3[:, :], col, None, ALU.is_equal)
                last.then_inc(s_hot, 1)

            def accumulate(l, c, g, s):
                b = dve.value_load(base_i[0:1, bass.ds(g, 1)], min_val=0, max_val=NODES)
                dve.wait_ge(s_back, c + 1)
                if not (isinstance(c, int) and c < 1):
                    dve.wait_ge(s_acc, c)
                n = 3 if l == 0 else 2
                window = agg[:, 0:n, bass.ds(b, WIN)]
                dve.tensor_tensor(out=window, in0=window,
                                  in1=PO[:, s, 3 * P:3 * P + n * WIN].rearrange("p (h w) -> p h w", w=WIN),
                                  op=ALU.add).then_inc(s_acc, 1)

            def stage(g, u):
                dve.tensor_copy(idx[:, (u - 1) * TILES:(u + 1) * TILES],
                                src_t[:, bass.ds((g - 1 + UNROLL) * TILES, 2 * TILES)]).then_inc(s_idx, 1)

            def edge_step(l, i, u, behind=True):
                g = i * UNROLL + u
                c = l * GROUPS + g
                if behind:
                    accumulate(l, c - 3, g - 3, (u + 1) % 2)
                dve.wait_ge(s_G[u], (l * (GROUPS // UNROLL) + i + 1) * TILES * 16)
                dve.wait_ge(s_X, c + 1)
                if not (isinstance(c, int) and c < 2):
                    dve.wait_ge(s_seg, c - 1)
                dve.tensor_tensor(out=M[:, u % 2, :],
                                  in0=PX[:, 2 * (u % 2):2 * (u % 2) + 2, :].rearrange("p b f -> p (b f)"),
                                  in1=G[:, u, :], op=ALU.add).then_inc(s_add, 1)
                build_hot(c + 2, g + 2, u % 2, (u + 2) % UNROLL)
                if u % 2:
                    stage(g, u)

            def statistics(k, n):
                for t in range(CT):
                    last = dve.bn_stats(st4[:, t, :], y_b[:, t * D:(t + 1) * D])
                last.then_inc(s_bn, 1)
                dve.wait_ge(s_bn, 2 * n + 1)
                dve.tensor_copy(stats[:, bass.ds(k * CT, CT), :], st4[:, :, :])
                dve.tensor_copy(inv[:, chunk(k)], y_b).then_inc(s_bn, 1)
                dve.wait_ge(s_bn, 2 * n + 2)

            def inverse_std(n):
                me, se, mo, so = (stats[:, :, i] for i in (1, 2, 4, 5))
                b = 9 * n
                dve.tensor_tensor(out=mean[:, :], in0=me, in1=mo, op=ALU.add).then_inc(s_nt, 1)
                dve.tensor_tensor(out=veps[:, :], in0=se, in1=so, op=ALU.add).then_inc(s_nt, 1)
                dve.tensor_tensor(out=rstd[:, :], in0=me, in1=mo, op=ALU.subtract).then_inc(s_nt, 1)
                dve.wait_ge(s_nt, b + 3)
                dve.tensor_scalar(mean[:, :], mean[:, :], 0.5, None, ALU.mult)
                dve.tensor_scalar(veps[:, :], veps[:, :], 1.0 / D, EPS, ALU.mult, ALU.add)
                dve.scalar_tensor_tensor(out=std[:, :], in0=rstd[:, :], scalar=0.25, in1=rstd[:, :],
                                         op0=ALU.mult, op1=ALU.mult).then_inc(s_nt, 1)
                dve.wait_ge(s_nt, b + 4)
                dve.tensor_tensor(out=veps[:, :], in0=veps[:, :], in1=std[:, :], op=ALU.add).then_inc(s_var, 1)
                dve.wait_ge(s_var, n + 1)
                dve.wait_ge(s_std, n + 1)
                dve.reciprocal(rstd[:, :], std[:, :]).then_inc(s_nt, 1)
                dve.wait_ge(s_nt, b + 5)
                dve.tensor_tensor(out=rstd[:, :], in0=rstd[:, :], in1=veps[:, :], op=ALU.mult).then_inc(s_nt, 1)
                dve.wait_ge(s_nt, b + 6)
                dve.tensor_tensor(out=rstd[:, :], in0=rstd[:, :], in1=std[:, :], op=ALU.add).then_inc(s_nt, 1)
                dve.wait_ge(s_nt, b + 7)
                dve.tensor_scalar(rstd[:, :], rstd[:, :], 0.5, None, ALU.mult).then_inc(s_nt, 1)
                dve.wait_ge(s_nt, b + 8)
                dve.reciprocal(rstd[:, :], rstd[:, :]).then_inc(s_nt, 1)
                dve.wait_ge(s_nt, b + 9)

            def normalise(k, tiles):
                for t in range(tiles):
                    row = inv[:, bass.ds((k * CT + t) * D, D)]
                    last = dve.tensor_scalar(row, row, mean[:, bass.ds(k * CT + t, 1)],
                                             rstd[:, bass.ds(k * CT + t, 1)], ALU.subtract, ALU.mult)
                return last

            def means(l, k):
                kk = l * CHUNKS + k
                dve.wait_ge(s_z, kk + 1)
                dve.scalar_tensor_tensor(out=t_b, in0=agg[:, 2, chunk(k)], scalar=b2_col[:, l:l + 1],
                                         in1=PX[:, 0, :], op0=ALU.mult, op1=ALU.add).then_inc(s_t, 1)
                dve.wait_ge(s_t, 1 + kk + 1)
                dve.tensor_tensor(out=m_b, in0=t_b, in1=inv[:, chunk(k)], op=ALU.mult).then_inc(s_m, 1)

            def node_step(l, k, first=False, last=False):
                kk = l * CHUNKS + k
                if not last:
                    if l == 0:
                        dve.wait_ge(s_inv, k + 2)
                    means(l, k + 1)
                if l < LAYERS - 1:
                    if not first:
                        split_A(l + 1, k - 1)
                    dve.wait_ge(s_v, kk + 1)
                    dve.tensor_scalar(r_b, PX[:, 3, :], c2_col[:, l:l + 1], 0.0, ALU.add, ALU.max).then_inc(s_r, 1)
                    dve.wait_ge(s_r, kk + 1)
                    if l == 0:
                        if not first:
                            dve.wait_ge(s_keep, k)
                        dve.wait_ge(s_prc, k + 1)
                        dve.scalar_tensor_tensor(out=h_b, in0=xres, scalar=pb_col[:, 0:1],
                                                 in1=r_b, op0=ALU.add, op1=ALU.add).then_inc(s_h, 1)
                    else:
                        dve.wait_ge(s_keep, CHUNKS)
                        dve.tensor_tensor(out=h_b, in0=hT[:, chunk(k)], in1=r_b, op=ALU.add).then_inc(s_h, 1)
                    if l == 0 and not (isinstance(k, int) and k >= CHUNKS - 2):
                        dve.reciprocal(inv[:, bass.ds((k + 2) * CHUNK, CHUNK)],
                                       inv[:, bass.ds((k + 2) * CHUNK, CHUNK)]).then_inc(s_inv, 1)
                else:
                    dve.wait_ge(s_v, kk + 1)
                    dve.wait_ge(s_xres, 16 * (k + 1))
                    by_node = lambda b: b.rearrange("p (t d) -> p t d", d=D)
                    dve.tensor_tensor(out=by_node(r_b), in0=by_node(PX[:, 3, :]),
                                      in1=c2_bc[:, :].unsqueeze(1).to_broadcast([P, CT, D]),
                                      op=ALU.add).then_inc(s_r, 1)
                    dve.wait_ge(s_r, kk + 1)
                    dve.tensor_tensor(out=y_b, in0=r_b, in1=xres, op=ALU.add).then_inc(s_y, 1)
                    dve.wait_ge(s_y, k + 1)
                    statistics(k, k)

            split_A(0, 0)
            with dve.Fori(1, CHUNKS, 1) as k:
                split_A(0, k)
            build_hot(0, 0, 0, 0)
            build_hot(1, 1, 1, 1)
            for l in range(LAYERS):
                dve.wait_ge(s_zero, 1 + 2 * l * CHUNKS)
                for half in range(2):
                    dve.wait_ge(s_store[half], (l + 1) * CHUNKS * 32)
                for u in range(UNROLL):
                    edge_step(l, 0, u, behind=u >= 3)
                with dve.Fori(1, GROUPS // UNROLL, 1) as i:
                    for u in range(UNROLL):
                        edge_step(l, i, u)
                for n in (3, 2, 1):
                    accumulate(l, (l + 1) * GROUPS - n, GROUPS - n, n % 2)
                far_edges(l)
                if l == 0:
                    dve.wait_ge(s_acc, GROUPS)
                    dve.tensor_scalar(inv[:, :], agg[:, 2, :], 1.0, None, ALU.max).then_inc(s_t, 1)
                    dve.wait_ge(s_t, 1)
                if l == 0:
                    for k in range(2):
                        dve.reciprocal(inv[:, chunk(k)], inv[:, chunk(k)]).then_inc(s_inv, 1)
                    dve.wait_ge(s_inv, 1)
                means(l, 0)
                node_step(l, 0, first=True)
                with dve.Fori(1, CHUNKS - 2, 1) as k:
                    node_step(l, k)
                node_step(l, CHUNKS - 2)
                node_step(l, CHUNKS - 1, last=True)
                if l < LAYERS - 1:
                    split_A(l + 1, CHUNKS - 1)
            inverse_std(0)
            hf = PX[:, 1, :].rearrange("p (t d) -> p t d", d=D)

            def x1_rows(k):
                normalise(k, CT).then_inc(s_nx, 1)
                dve.wait_ge(s_nx, k + 1)
                dve.tensor_copy(x_b, inv[:, chunk(k)]).then_inc(s_x1, 1)

            def first_part(k):
                dve.wait_ge(s_hf, k + 1)
                dve.wait_ge(s_xres, (CHUNKS + k) * 16)
                dve.tensor_copy(H3st[:, :, 0, :], hf).then_inc(s_hs, 1)

            def remainder(k):
                dve.wait_ge(s_hs, 3 * k + 1)
                dve.tensor_tensor(out=xres_t, in0=hf, in1=H3st[:, :, 0, :], op=ALU.subtract).then_inc(s_hs, 1)

            def second_part(k):
                dve.wait_ge(s_hs, 3 * k + 2)
                dve.tensor_copy(H3st[:, :, 1, :], xres_t).then_inc(s_hs, 1)

            def shifted_softplus(c, s):
                dve.wait_ge(s_abs, c + 1)
                if not (isinstance(c, int) and c < 1):
                    dve.wait_ge(s_sp, c)
                dve.tensor_scalar(q_b, PX[:, s, :], bf1_col[:, 0:1], 0.0, ALU.add, ALU.max).then_inc(s_q, 1)
                dve.wait_ge(s_q, c + 1)
                dve.wait_ge(s_ln, c + 1)
                if not (isinstance(c, int) and c < 2):
                    dve.wait_ge(s_Y, c - 1)
                dve.scalar_tensor_tensor(out=sp_b[:, s, :], in0=q_b, scalar=-LOG2, in1=l_b,
                                         op0=ALU.add, op1=ALU.add).then_inc(s_sp, 1)

            steps = [0]

            def after(ins):
                steps[0] += 1
                ins.then_inc(s_rt, 1)
                dve.wait_ge(s_rt, steps[0])

            source = src_t[:, 0:GROUPS * TILES]
            after(dve.tensor_scalar(place_i, source, 7, None, ALU.arith_shift_right))
            after(dve.tensor_copy(bucket_f, place_i))
            dve.tensor_copy(iota_bb, iota_b[:, :])
            after(dve.tensor_copy(bucket_b, bucket_f))
            after(dve.scalar_tensor_tensor(out=loc_f, in0=bucket_f, scalar=-float(P), in1=source,
                                           op0=ALU.mult, op1=ALU.add))
            same_b = place_f.bitcast(BF16)[:, 0:GROUPS * TILES]
            for b in range(NB):
                dve.tensor_scalar(same_b, bucket_b, float(b), 0.0, ALU.is_equal, ALU.add,
                                  accum_out=many[:, b:b + 1]).then_inc(s_cnt, 1)
                dve.wait_ge(s_cnt, b + 1)
            dve.wait_ge(s_tot, 1)
            after(dve.tensor_scalar(groups_i, PX[:, 0, 0:NB], float(GROUP - 1), None, ALU.add))
            after(dve.tensor_scalar(groups_i, groups_i, 9, None, ALU.arith_shift_right))
            after(dve.tensor_copy(groups_b, groups_i))
            summed, d, pair = groups_b, 1, [ends, ends2]
            while d < NB:
                dve.tensor_copy(pair[0][:, 0:d], summed[:, 0:d])
                after(dve.tensor_tensor(out=pair[0][:, d:NB], in0=summed[:, d:NB], in1=summed[:, 0:NB - d], op=ALU.add))
                summed, d, pair = pair[0], 2 * d, pair[::-1]
            assert summed is ends_last
            after(dve.tensor_tensor(out=starts, in0=summed, in1=groups_b, op=ALU.subtract))
            after(dve.tensor_scalar(starts, starts, float(GROUP), None, ALU.mult))
            dve.tensor_scalar(full, groups_b, 1.0, None, ALU.min).then_inc(s_start, 1)
            dve.wait_ge(s_start, 1)
            head = zero_list_f[:, 0:NB]
            dve.wait_ge(s_zero, 3 + (2 * LAYERS - 1) * CHUNKS)
            after(dve.scalar_tensor_tensor(out=head, in0=summed, scalar=-float(SPARE + 1), in1=iota_b[:, :],
                                           op0=ALU.add, op1=ALU.subtract))
            after(dve.tensor_tensor(out=head, in0=head, in1=full, op=ALU.mult))
            after(dve.scalar_tensor_tensor(out=head, in0=head, scalar=float(SPARE), in1=iota_b[:, :],
                                           op0=ALU.add, op1=ALU.add))
            after(dve.tensor_scalar(zero_list_f[:, NB:NB + TAIL], iota_t[:, 0:TAIL], summed[:, NB - 1:NB],
                                    None, ALU.add))
            dve.tensor_copy(zero_list[0:1, :], zero_list_f[0:1, :]).then_inc(s_list, 1)
            dve.wait_ge(s_run, 1)
            after(dve.tensor_copy(col_end[0:NB, :], PX[0:NB, 2, 0:1]))
            dve.tensor_scalar(M[0:NB, 0, 0:SORTED], iota_t[0:NB, :], col_end[0:NB, :], None,
                              ALU.is_ge).then_inc(s_mask, 1)
            dve.wait_ge(s_tb, 1)
            after(dve.tensor_scalar(node_base[0:1, :], PX[0:1, 2, 0:SORTED], float(P), None, ALU.mult))

            by_step = bucket_f.rearrange("p (s t) -> p s t", t=STEP)
            earlier = M[:, 1, 0:GROUPS * TILES]
            earlier_s = earlier.rearrange("p (s t) -> p s t", t=STEP)
            after(dve.memset(earlier, 0.0))
            for d in range(1, STEP):
                same = M[:, 0, 0:STEPS * (STEP - d)].rearrange("p (s t) -> p s t", t=STEP - d)
                after(dve.tensor_tensor(out=same, in0=by_step[:, :, d:STEP], in1=by_step[:, :, 0:STEP - d],
                                        op=ALU.is_equal))
                after(dve.tensor_tensor(out=earlier_s[:, :, d:STEP], in0=earlier_s[:, :, d:STEP], in1=same,
                                        op=ALU.add))

            def build_buckets(n, s):
                if not (isinstance(n, int) and n < 4):
                    dve.wait_ge(s_cum, n - 3)
                    dve.wait_ge(s_mul, n - 3)
                dve.tensor_tensor(
                    out=one_bucket[:, s, :, :],
                    in0=bucket_b[:, bass.ds(n * STEP, STEP)].unsqueeze(2).to_broadcast([P, STEP, NB]),
                    in1=iota_bb.unsqueeze(1).to_broadcast([P, STEP, NB]),
                    op=ALU.is_equal).then_inc(s_ob, 1)

            def pick_places(n, s):
                dve.wait_ge(s_mul, n + 1)
                dve.tensor_reduce(out=place_f[:, bass.ds(n * STEP, STEP)], in_=picked[:, s, :, :],
                                  axis=mybir.AxisListType.X, op=ALU.add).then_inc(s_pick, 1)

            def steps_of_chunk(k, first=False, last=False):
                for n in range(PER_CHUNK):
                    at = k * PER_CHUNK + n
                    if not (last and n >= PER_CHUNK - 2):
                        build_buckets(at + 2, (n + 2) % 4)
                    if not (first and n == 0):
                        pick_places(at - 1, (n - 1) % 2)
                    if n == 3:
                        first_part(k)
                    if n == 4:
                        remainder(k)
                    if n == 5:
                        second_part(k)
                    if n == 6 and not last:
                        x1_rows(k + 1)

            x1_rows(0)
            build_buckets(0, 0)
            build_buckets(1, 1)
            steps_of_chunk(0, first=True)
            with dve.Fori(1, CHUNKS - 1, 1) as k:
                steps_of_chunk(k)
            steps_of_chunk(CHUNKS - 1, last=True)
            pick_places(STEPS - 1, 1)
            dve.wait_ge(s_pick, STEPS)
            dve.wait_ge(s_cum, STEPS)
            dve.tensor_tensor(out=place_i, in0=place_f, in1=earlier, op=ALU.add).then_inc(s_place, 1)

            def filter_step(i, u):
                g = i * UNROLL + u
                c = LAYERS * GROUPS + g
                landed = (LAYERS * (GROUPS // UNROLL) + i) * TILES * 16
                if u % 2 == 0:
                    dve.wait_ge(s_G[u], landed)
                    dve.wait_ge(s_G[u + 1], landed)
                    dve.tensor_copy(idx[:, u * TILES:(u + 2) * TILES],
                                    place_i[:, bass.ds(g * TILES, 2 * TILES)]).then_inc(s_idx, 1)
                build_hot(c + 2, g + 2, u % 2, 0, sums=False)
                shifted_softplus(g + 1, (u + 1) % 2)
                dve.wait_ge(s_xj, g + 1)
                dve.wait_ge(s_Y, g + 1)
                for j in range(TILES):
                    t = bass.ds(g * TILES + j, 1)
                    dve.scalar_tensor_tensor(out=rows[:, u, j, 0:D], in0=xj_b[:, u % 2, j * D:(j + 1) * D],
                                             scalar=rcut_t[:, t], in1=PX[:, 2 + u % 2, j * D:(j + 1) * D],
                                             op0=ALU.mult, op1=ALU.mult)
                dve.tensor_copy(rows[:, u, :, D], loc_f[:, bass.ds(g * TILES, TILES)]).then_inc(s_prod, 1)

            dve.wait_ge(s_rcut, 16)
            dve.wait_ge(s_place, 1)
            far_filter_rows()
            shifted_softplus(0, 0)
            for u in range(UNROLL):
                filter_step(0, u)
            with dve.Fori(1, GROUPS // UNROLL, 1) as i:
                for u in range(UNROLL):
                    filter_step(i, u)

            def sorted_step(i, u, behind=True):
                g = i * SLOTS + u
                dve.wait_ge(s_row[u], 16 * (i + 1))
                if not (isinstance(g, int) and g < 2):
                    dve.wait_ge(s_seg1, g - 1)
                dve.tensor_tensor(out=hot128[:, u % 2, :, :],
                                  in0=iota_t[:, 0:P].unsqueeze(1).to_broadcast([P, TILES, P]),
                                  in1=sorted_rows[:, u, :, D:ROW].to_broadcast([P, TILES, P]),
                                  op=ALU.is_equal).then_inc(s_hot128, 1)
                if behind:
                    add_sorted(g - 2, (u - 2) % 3)

            def add_sorted(g, s):
                b = dve.value_load(node_base[0:1, bass.ds(g, 1)], min_val=0, max_val=NB * P)
                dve.wait_ge(s_seg1, g + 1)
                if not (isinstance(g, int) and g < 1):
                    dve.wait_ge(s_acc1, g)
                window = agg[:, 0, bass.ds(b, P)]
                dve.tensor_tensor(out=window, in0=window, in1=PX[:, s, 0:P], op=ALU.add).then_inc(s_acc1, 1)

            for u in range(SLOTS):
                sorted_step(0, u, behind=u >= 2)
            with dve.Fori(1, SORTED // SLOTS, 1) as i:
                for u in range(SLOTS):
                    sorted_step(i, u)
            add_sorted(SORTED - 2, 1)
            add_sorted(SORTED - 1, 2)

            def out_softplus(k, first=False):
                if not first:
                    dve.wait_ge(s_osp, k)
                dve.wait_ge(s_oa, 3 * k + 1)
                dve.tensor_scalar(r_b, PX[:, 0, :], bo1_col[:, 0:1], 0.0, ALU.add, ALU.max).then_inc(s_ot, 1)
                dve.wait_ge(s_ot, k + 1)
                dve.wait_ge(s_oa, 3 * k + 3)
                if not first:
                    dve.wait_ge(s_o2, k)
                dve.scalar_tensor_tensor(out=sp_b[:, 0, :], in0=r_b, scalar=-LOG2, in1=xres,
                                         op0=ALU.add, op1=ALU.add).then_inc(s_osp, 1)

            def out_rows(k):
                dve.wait_ge(s_o2, k + 1)
                yk = y_b.rearrange("p (t d) -> p t d", d=D)
                dve.tensor_tensor(out=y_b, in0=inv[:, chunk(k)], in1=PX[:, 3, :], op=ALU.add).then_inc(s_oy, 1)
                dve.wait_ge(s_oy, k + 1)
                dve.tensor_tensor(out=yk, in0=yk, in1=bo2_bc[:, :].unsqueeze(1).to_broadcast([P, CT, D]),
                                  op=ALU.add).then_inc(s_y2, 1)
                dve.wait_ge(s_y2, k + 1)
                statistics(k, CHUNKS + k)

            out_softplus(0, first=True)
            with dve.Fori(1, CHUNKS, 1) as k:
                out_softplus(k)
                out_rows(k - 1)
            out_rows(CHUNKS - 1)
            inverse_std(1)
            with dve.Fori(0, FULL_TILES // CT, 1) as k:
                normalise(k, CT).then_inc(s_norm, 1)
            normalise(FULL_TILES // CT, 1).then_inc(s_norm, 1)


def kernel(**inputs):
    import numpy as _np
    import concourse.bacc as _bacc
    from concourse import mybir as _mybir
    from concourse.bass_utils import run_bass_kernel_spmd as _run

    a = {n: _np.ascontiguousarray(v) for n, v in inputs.items()}

    def edge_table(v, pad):
        whole = _np.full(GROUPS * GROUP, pad, v.dtype)
        whole[:EDGES] = v
        t = whole.reshape(GROUPS * TILES, P).T
        return _np.ascontiguousarray(_np.concatenate([t, t[:, :AHEAD * TILES]], axis=1))

    xN = _np.zeros((NPAD, D), a["x"].dtype)
    xN[:NODES] = a["x"]
    fT = _np.zeros((RBF, (GROUPS + 1) * GROUP), a["edge_attr_20"].dtype)
    fT[:, :EDGES] = a["edge_attr_20"].T
    c0 = lambda v: _np.ascontiguousarray(v)
    laid = {
        "xT": c0(xN.T), "xN": xN,
        "src": edge_table(a["src"], 0), "dst": edge_table(a["dst"], -1),
        "rcut": edge_table(a["edge_weight"], 0), "fT": fT,
        "phi_w1": a["L0_gnn_phi_w1"], "phi_b1": a["L0_gnn_phi_b1"], "phi_w2": a["L0_gnn_phi_w2"],
        "phi_b2": c0(a["L0_gnn_phi_b2"].T), "psi_w1": a["L0_gnn_psi_w1"],
        "psi_b1": c0(a["L0_gnn_psi_b1"].reshape(LAYERS, 2, P).transpose(2, 0, 1)),
        "psi_w2": a["L0_gnn_psi_w2"], "psi_b2": c0(a["L0_gnn_psi_b2"].T),
        "psi_b2_last": c0(a["L0_gnn_psi_b2"][LAYERS - 1:]),
        "proj_w": a["L0_gnn_proj_w"], "proj_b": a["L0_gnn_proj_b"].reshape(P, 1),
        "w_in2f": a["L1_gnn_W_in2f"], "w_f1": a["L1_gnn_W_f1"], "b_f1": a["L1_gnn_b_f1"].reshape(P, 1),
        "w_f2": a["L1_gnn_W_f2"], "b_f2": a["L1_gnn_b_f2"].reshape(1, D),
        "w_o1": a["L1_gnn_W_o1"], "b_o1": a["L1_gnn_b_o1"].reshape(P, 1),
        "w_o2": a["L1_gnn_W_o2"], "b_o2": a["L1_gnn_b_o2"].reshape(1, D),
    }
    nc = _bacc.Bacc("TRN2", target_bir_lowering=False, num_devices=1)
    arrays, args = {}, {}
    for name, v in laid.items():
        arrays[f"in_{name}"] = v
        args[name] = nc.dram_tensor(f"in_{name}", v.shape, _mybir.dt.from_np(v.dtype), kind="ExternalInput").ap()
    args["out"] = nc.dram_tensor("out_0", (NODES, D), _mybir.dt.float32, kind="ExternalOutput").ap()
    build(nc, **args)
    r = _run(nc, [arrays], core_ids=[0])
    return r.results[0]["out_0"]
```
